# Optimizing a Trainium2 kernel written in Bass

```python
import numpy as np
import jax
import jax.numpy as jnp

def _softmax(x, axis=-1):
    return jax.nn.softmax(x, axis=axis)

def _gelu(x):
    return jax.nn.gelu(x, approximate=True)

def _silu(x):
    return jax.nn.silu(x)

def _sigmoid(x):
    return jax.nn.sigmoid(x)

def _layernorm(x, axis=-1, eps=1e-05):
    m = jnp.mean(x, axis=axis, keepdims=True)
    v = jnp.var(x, axis=axis, keepdims=True)
    return (x - m) / jnp.sqrt(v + eps)

def _scatter_add(tgt, idx, src, axis=0):
    return tgt.at[idx].add(src)

def _segment_sum(src, seg, n):
    return jax.ops.segment_sum(src, seg, n)
kernel_name = 'mk_xattn_ffn_d2_seqx_r4_75a13c'

def setup_inputs(seed: int=0):
    np.random.seed(seed)
    _w = jnp.asarray

    def _rec_inputs():
        import jax
        import jax.numpy as jnp
        _rk = jax.random.key(seed)
        x = -0.000125 + 0.9999 * jax.random.normal(jax.random.fold_in(_rk, 1), (4, 512, 512), jnp.float32)
        _lenS = 512 - jax.random.randint(jax.random.fold_in(_rk, 7), (4,), 0, max(1, 512 // 4) + 1, jnp.int32)
        _lenS2 = 512 - jax.random.randint(jax.random.fold_in(_rk, 8), (4,), 0, max(1, 512 // 4) + 1, jnp.int32)
        itok_BxS_13_99985 = jax.random.randint(jax.random.fold_in(_rk, 11), (4, 512), 13, 99986, jnp.int32)
        _ctx_2048P = jax.random.normal(jax.random.fold_in(_rk, 12), (4, 16, 512), jnp.float32)
        _ctx_2048c = jax.random.dirichlet(jax.random.fold_in(_rk, 512), 0.3 * jnp.ones((16,), jnp.float32), (4, 512))
        _ctx_2048t = jnp.einsum('bsk,bkd->bsd', _ctx_2048c, _ctx_2048P)
        _ctx_2048t = _ctx_2048t * jax.lax.rsqrt(jnp.mean(jnp.square(_ctx_2048t)) + 1e-12) * 0.953939
        ctx_2048 = 6.82029e-06 + 0.0200006 * (_ctx_2048t + 0.3 * jax.random.normal(jax.random.fold_in(_rk, 612), (4, 512, 512), jnp.float32))
        return (x, itok_BxS_13_99985, ctx_2048)
    x, itok_BxS_13_99985, ctx_2048 = _rec_inputs()

    def _L0_xattn_setup():
        import jax, jax.numpy as jnp
        import numpy as np
        B, S, D = (4, 1024, 512)
        E = 4
        F = 2048 // E
        VOCAB = 25000
        key = jax.random.key(seed)
        k1, k2, k3, k4, k5 = jax.random.split(key, 5)
        hidden_states = jax.random.normal(k1, (B, S, D), dtype=jnp.float32)
        token_ids = jax.random.randint(k2, (B, S), 0, VOCAB, dtype=jnp.int64)
        Wg = jax.random.normal(k3, (E, F, D), dtype=jnp.float32) * 0.02
        Wu = jax.random.normal(k4, (E, F, D), dtype=jnp.float32) * 0.02
        Wd = jax.random.normal(k5, (E, D, F), dtype=jnp.float32) * 0.02
        return {'hidden_states': hidden_states, 'token_ids': token_ids, 'Wg': Wg, 'Wu': Wu, 'Wd': Wd}
    _L0_xattn_all = _L0_xattn_setup()
    _L0_xattn_in = {k: v for k, v in _L0_xattn_all.items() if k in ()}
    del _L0_xattn_all

    def _L0_ffn_setup():
        import jax, jax.numpy as jnp
        import numpy as np
        D_MODEL = 512
        HIDDEN = 4 * D_MODEL
        EPS = 1e-05
        QB = 127.0

        def _ste(orig, quant):
            return orig + jax.lax.stop_gradient(quant - orig)

        def _act_quant(a):
            scale = QB / jnp.clip(jnp.max(jnp.abs(a), axis=-1, keepdims=True), 1e-05)
            q = jnp.clip(jnp.round(a * scale), -QB, QB) / scale
            return _ste(a, q)

        def _weight_quant(w):
            s = jnp.clip(jnp.mean(jnp.abs(w)), 1e-05)
            q = jnp.clip(jnp.round(w / s), -1.0, 1.0) * s
            return _ste(w, q)

        def _bitlinear(x, w):
            return jnp.einsum('bsd,od->bso', _act_quant(x), _weight_quant(w))

        def _rmsnorm(x, g):
            var = jnp.mean(jnp.square(x), axis=-1, keepdims=True)
            return x * jax.lax.rsqrt(var + EPS) * g
        key = jax.random.key(seed)
        k1, k2, k3 = jax.random.split(key, 3)
        x = jax.random.normal(k1, (4, 512, D_MODEL), dtype=jnp.float32)
        norm_w = jnp.ones((D_MODEL,), dtype=jnp.float32)
        w_gv = jax.random.normal(k2, (2 * HIDDEN, D_MODEL), dtype=jnp.float32) * D_MODEL ** (-0.5)
        w_out = jax.random.normal(k3, (D_MODEL, HIDDEN), dtype=jnp.float32) * HIDDEN ** (-0.5)
        return {'x': x, 'norm_w': norm_w, 'w_gv': w_gv, 'w_out': w_out}
    _L0_ffn_all = _L0_ffn_setup()
    _L0_ffn_in = {k: v for k, v in _L0_ffn_all.items() if k in ('norm_w', 'w_gv', 'w_out')}
    del _L0_ffn_all

    def _L1_xattn_setup():
        import jax, jax.numpy as jnp
        import numpy as np
        EPS = 1e-06
        NUM_HEADS = 16

        def _feature_map(x):
            return jnp.where(x > 0, x + 1.0, jnp.exp(x))
        key = jax.random.key(seed)
        ks = jax.random.split(key, 7)
        B, L, S, D = (4, 1024, 1024, 512)
        sc = 1.0 / np.sqrt(D)
        return {'query': jax.random.normal(ks[0], (B, L, D), jnp.float32), 'kv': jax.random.normal(ks[1], (B, S, D), jnp.float32), 'Wq': jax.random.normal(ks[2], (D, D), jnp.float32) * sc, 'Wg': jax.random.normal(ks[3], (D, D), jnp.float32) * sc, 'bg': jnp.ones((D,), jnp.float32), 'Wkv': jax.random.normal(ks[4], (2 * D, D), jnp.float32) * sc, 'Wo': jax.random.normal(ks[5], (D, D), jnp.float32) * sc}
    _L1_xattn_all = _L1_xattn_setup()
    _L1_xattn_in = {k: v for k, v in _L1_xattn_all.items() if k in ('Wq', 'Wg', 'bg', 'Wkv', 'Wo')}
    del _L1_xattn_all

    def _L1_ffn_setup():
        import jax, jax.numpy as jnp
        import numpy as np
        B, S, H = (1, 512, 512)
        E, K, I = (16, 4, 352)
        IS = 704
        CAP = 256
        key = jax.random.key(seed)
        ks = jax.random.split(key, 8)
        sc = 0.02
        return {'hidden_states': jax.random.normal(ks[0], (B, S, H), jnp.float32), 'gate_w': jax.random.normal(ks[1], (E, H), jnp.float32) * sc, 'w_gate': jax.random.normal(ks[2], (E, H, I), jnp.float32) * sc, 'w_up': jax.random.normal(ks[3], (E, H, I), jnp.float32) * sc, 'w_down': jax.random.normal(ks[4], (E, I, H), jnp.float32) * sc, 'sw_gate': jax.random.normal(ks[5], (H, IS), jnp.float32) * sc, 'sw_up': jax.random.normal(ks[6], (H, IS), jnp.float32) * sc, 'sw_down': jax.random.normal(ks[7], (IS, H), jnp.float32) * sc}
    _L1_ffn_all = _L1_ffn_setup()
    _L1_ffn_in = {k: v for k, v in _L1_ffn_all.items() if k in ('gate_w', 'w_gate', 'w_up', 'w_down', 'sw_gate', 'sw_up', 'sw_down')}
    del _L1_ffn_all
    return {'x': x, 'itok_BxS_13_99985': itok_BxS_13_99985, 'ctx_2048': ctx_2048, 'L0_ffn_norm_w': _L0_ffn_in['norm_w'], 'L0_ffn_w_gv': _L0_ffn_in['w_gv'], 'L0_ffn_w_out': _L0_ffn_in['w_out'], 'L1_xattn_Wq': _L1_xattn_in['Wq'], 'L1_xattn_Wg': _L1_xattn_in['Wg'], 'L1_xattn_bg': _L1_xattn_in['bg'], 'L1_xattn_Wkv': _L1_xattn_in['Wkv'], 'L1_xattn_Wo': _L1_xattn_in['Wo'], 'L1_ffn_gate_w': _L1_ffn_in['gate_w'], 'L1_ffn_w_gate': _L1_ffn_in['w_gate'], 'L1_ffn_w_up': _L1_ffn_in['w_up'], 'L1_ffn_w_down': _L1_ffn_in['w_down'], 'L1_ffn_sw_gate': _L1_ffn_in['sw_gate'], 'L1_ffn_sw_up': _L1_ffn_in['sw_up'], 'L1_ffn_sw_down': _L1_ffn_in['sw_down']}

def reference(x, itok_BxS_13_99985, ctx_2048, L0_ffn_norm_w, L0_ffn_w_gv, L0_ffn_w_out, L1_xattn_Wq, L1_xattn_Wg, L1_xattn_bg, L1_xattn_Wkv, L1_xattn_Wo, L1_ffn_gate_w, L1_ffn_w_gate, L1_ffn_w_up, L1_ffn_w_down, L1_ffn_sw_gate, L1_ffn_sw_up, L1_ffn_sw_down):
    import jax
    import jax.numpy as jnp

    def _L0_xattn_ref(hidden_states, token_ids, Wg, Wu, Wd):
        import jax, jax.numpy as jnp
        import numpy as np
        B, S, D = (4, 1024, 512)
        E = 4
        F = 2048 // E
        VOCAB = 25000
        tokens_per_expert = VOCAB // E
        tid = jnp.clip(token_ids, 0, VOCAB - 1)
        expert_ids = jnp.minimum(tid // tokens_per_expert, E - 1)
        out = jnp.zeros_like(hidden_states)
        for e in range(E):
            g = jax.nn.silu(jnp.einsum('bsd,fd->bsf', hidden_states, Wg[e]))
            u = jnp.einsum('bsd,fd->bsf', hidden_states, Wu[e])
            y = jnp.einsum('bsf,df->bsd', g * u, Wd[e])
            out = jnp.where((expert_ids == e)[..., None], y, out)
        return out

    def _L0_ffn_ref(x, norm_w, w_gv, w_out):
        import jax, jax.numpy as jnp
        import numpy as np
        D_MODEL = 512
        HIDDEN = 4 * D_MODEL
        EPS = 1e-05
        QB = 127.0

        def _ste(orig, quant):
            return orig + jax.lax.stop_gradient(quant - orig)

        def _act_quant(a):
            scale = QB / jnp.clip(jnp.max(jnp.abs(a), axis=-1, keepdims=True), 1e-05)
            q = jnp.clip(jnp.round(a * scale), -QB, QB) / scale
            return _ste(a, q)

        def _weight_quant(w):
            s = jnp.clip(jnp.mean(jnp.abs(w)), 1e-05)
            q = jnp.clip(jnp.round(w / s), -1.0, 1.0) * s
            return _ste(w, q)

        def _bitlinear(x, w):
            return jnp.einsum('bsd,od->bso', _act_quant(x), _weight_quant(w))

        def _rmsnorm(x, g):
            var = jnp.mean(jnp.square(x), axis=-1, keepdims=True)
            return x * jax.lax.rsqrt(var + EPS) * g
        residual = x
        h = _rmsnorm(x, norm_w)
        gv = _bitlinear(h, w_gv)
        value, gate = jnp.split(gv, 2, axis=-1)
        h = value * jax.nn.silu(gate)
        h = _bitlinear(h, w_out)
        return residual + h

    def _L1_xattn_ref(query, kv, Wq, Wg, bg, Wkv, Wo):
        import jax, jax.numpy as jnp
        import numpy as np
        EPS = 1e-06
        NUM_HEADS = 16

        def _feature_map(x):
            return jnp.where(x > 0, x + 1.0, jnp.exp(x))
        B, L, D = query.shape
        S = kv.shape[1]
        H = NUM_HEADS
        hd = D // H
        q = query @ Wq.T
        gate = jax.nn.sigmoid(query @ Wg.T + bg)
        kvp = kv @ Wkv.T
        k, v = jnp.split(kvp, 2, axis=-1)
        q = _feature_map(q.reshape(B, L, H, hd).transpose(0, 2, 1, 3))
        k = _feature_map(k.reshape(B, S, H, hd).transpose(0, 2, 1, 3))
        v = v.reshape(B, S, H, hd).transpose(0, 2, 1, 3)
        kv_summary = jnp.einsum('bhsd,bhse->bhde', k, v)
        k_sum = k.sum(axis=-2)
        z = 1.0 / (jnp.einsum('bhld,bhd->bhl', q, k_sum)[..., None] + EPS)
        attn = jnp.einsum('bhld,bhde->bhle', q, kv_summary) * z
        attn = attn.transpose(0, 2, 1, 3).reshape(B, L, D)
        out = attn * gate @ Wo.T
        return out

    def _L1_ffn_ref(hidden_states, gate_w, w_gate, w_up, w_down, sw_gate, sw_up, sw_down):
        import jax, jax.numpy as jnp
        import numpy as np
        B, S, H = (1, 512, 512)
        E, K, I = (16, 4, 352)
        IS = 704
        CAP = 256
        b, s, h = hidden_states.shape
        x = hidden_states.reshape(-1, h)
        T = x.shape[0]
        scores = jax.nn.softmax(x @ gate_w.T, axis=-1)
        topk_w, topk_i = jax.lax.top_k(scores, K)
        topk_w = topk_w / (topk_w.sum(-1, keepdims=True) + 1e-20)
        flat_i = topk_i.reshape(-1)
        flat_w = topk_w.reshape(-1)
        order = jnp.argsort(flat_i)
        se = flat_i[order]
        counts = jax.ops.segment_sum(jnp.ones_like(flat_i), flat_i, num_segments=E)
        starts = jnp.cumsum(counts) - counts
        rank = jnp.arange(T * K) - starts[se]
        tok = order // K
        slot = jnp.where(rank < CAP, rank, CAP)
        buf = jnp.full((E, CAP + 1), T, dtype=jnp.int32).at[se, slot].set(tok)[:, :CAP]
        wbuf = jnp.zeros((E, CAP + 1), x.dtype).at[se, slot].set(flat_w[order])[:, :CAP]
        xpad = jnp.concatenate([x, jnp.zeros((1, h), x.dtype)], axis=0)
        xg = xpad[buf]
        gact = jax.nn.silu(jnp.einsum('ech,ehi->eci', xg, w_gate))
        mid = gact * jnp.einsum('ech,ehi->eci', xg, w_up)
        eout = jnp.einsum('eci,eih->ech', mid, w_down) * wbuf[..., None]
        y = jnp.zeros((T + 1, h), x.dtype).at[buf.reshape(-1)].add(eout.reshape(-1, h))[:T]
        shared = jax.nn.silu(x @ sw_gate) * (x @ sw_up) @ sw_down
        return (y + shared).reshape(b, s, h)
    x = x + _L0_xattn_ref(_layernorm(x, axis=-1), itok_BxS_13_99985, ctx_2048, ctx_2048, ctx_2048)
    x = x + _L0_ffn_ref(_layernorm(x, axis=-1), L0_ffn_norm_w, L0_ffn_w_gv, L0_ffn_w_out)
    x = x + _L1_xattn_ref(_layernorm(x, axis=-1), ctx_2048, L1_xattn_Wq, L1_xattn_Wg, L1_xattn_bg, L1_xattn_Wkv, L1_xattn_Wo)
    x = x + _L1_ffn_ref(_layernorm(x, axis=-1), L1_ffn_gate_w, L1_ffn_w_gate, L1_ffn_w_up, L1_ffn_w_down, L1_ffn_sw_gate, L1_ffn_sw_up, L1_ffn_sw_down)
    return x

_drawn_inputs = setup_inputs


def setup_inputs(seed=0):
    import zlib

    import numpy as np

    out = dict(_drawn_inputs(seed))
    spreads = {'L0_ffn_norm_w': (1.0, 0.6), 'L1_xattn_bg': (1.0, 0.6)}
    factors = {'L1_xattn_Wq': 8.0,
     'L1_xattn_Wg': 8.0,
     'L1_xattn_Wkv': 8.0,
     'L1_xattn_Wo': 8.0,
     'L1_ffn_gate_w': 8.0,
     'L1_ffn_w_gate': 7.748,
     'L1_ffn_w_up': 7.566,
     'L1_ffn_w_down': 7.573,
     'L1_ffn_sw_gate': 8.0,
     'L1_ffn_sw_up': 8.0,
     'L1_ffn_sw_down': 8.0}
    for name, (base, spread) in spreads.items():
        noise = np.random.default_rng([zlib.crc32(name.encode()), seed]).standard_normal(out[name].shape)
        drawn = base * np.exp(spread * noise) if base else spread * noise
        out[name] = jnp.asarray(drawn.astype(out[name].dtype))
    for name, factor in factors.items():
        out[name] = (out[name] * factor).astype(out[name].dtype)
    return out
```

```python
from contextlib import ExitStack

import numpy as np
import concourse.bass as bass
from concourse import mybir

fp32, f32r, bf16, i32 = mybir.dt.float32, mybir.dt.float32r, mybir.dt.bfloat16, mybir.dt.int32
ALU, ACT, AX = mybir.AluOpType, mybir.ActivationFunctionType, mybir.AxisListType

P = 128
B, S, D = 4, 512, 512
T = B * S
TT = T // P
KD = D // P
LN_EPS = 1e-5
E0, VOCAB = 4, 25000
PER_EXPERT = VOCAB // E0
SORTED = TT + E0
AHEAD = 2
HID = 2048
QB = 127.0
MAGIC = 12582912.0
HEADS = 16
HD = D // HEADS
ATT_EPS = 1e-6
E1, TOPK, FF, CAP = 16, 4, 352, 256
FT = 3
FLAST = FF - 2 * P
ST = CAP // P
SLOTS = E1 * ST
SFF = 704
SFT = 6
SLAST = SFF - 5 * P
NOWHERE = 4096.0


class Shared:
    pass


def at(i, per, j=0):
    return i * per + (j + 1)


def mm3(pe, out, lhs, rhs, first, last):
    (ah, al), (bh, bl) = lhs, rhs
    pe.matmul(out, ah, bh, start=first, stop=False)
    pe.matmul(out, ah, bl, start=False, stop=False)
    return pe.matmul(out, al, bh, start=False, stop=last)


def f(ap):
    return ap.bitcast(fp32)


def constants(nc, g, ctx):
    def sb(name, shape, dt):
        return ctx.enter_context(nc.sbuf_tensor(name, shape, dt))
    g.bank = [ctx.enter_context(nc.psum_tensor(f"bank{n}", [P, 512], fp32)) for n in range(8)]
    g.ident = sb("ident", [P, P], fp32)
    g.ident_b = sb("ident_b", [P, P], bf16)
    g.before_b = sb("before_b", [P, P], bf16)
    g.ones_b = sb("ones_b", [P, P], bf16)
    g.ones_r = sb("ones_r", [P, P], f32r)
    g.headmask = sb("headmask", [P, P], fp32)
    g.ramp = sb("ramp", [P, P], fp32)
    g.token_less = sb("token_less", [P, TT], fp32)
    g.minus_half = sb("minus_half", [P, 2 * KD], fp32)
    g.zeros = sb("zeros", [P, 32], fp32)
    g.kramp = sb("kramp", [P, TOPK], fp32)
    g.spare = sb("spare", [P, 1], fp32)
    g.slot_base = sb("slot_base", [P, E1], fp32)
    g.sorted_idx = sb("sorted_idx", [P, SORTED + AHEAD], i32)
    g.tile_expert = sb("tile_expert", [1, SORTED + AHEAD], i32)
    g.pos = sb("pos", [P, TT], i32)
    g.wscale = sb("wscale", [P, 2], fp32)
    g.whalf = sb("whalf", [P, 4], fp32)
    made = ctx.enter_context(nc.semaphore("constants_made"))
    step = ctx.enter_context(nc.semaphore("constants_step"))
    with nc.Block() as block:
        @block.gpsimd
        def _(gp):
            gp.memset(g.ident[:, :], 0.0)
            gp.memset(g.ident_b[:, :], 0.0)
            gp.memset(g.before_b[:, :], 1.0)
            gp.memset(g.ones_b[:, :], 1.0)
            gp.memset(f(g.ones_r[:, :]), 1.0)
            gp.memset(g.headmask[:, :], 1.0)
            gp.memset(g.minus_half[:, :], -0.5)
            gp.memset(g.zeros[:, :], 0.0)
            gp.iota(g.ramp[:, :], [[1, P]], base=0, channel_multiplier=0, allow_small_or_imprecise_dtypes=True)
            gp.iota(g.spare[:, :], [[1, 1]], base=T, channel_multiplier=1, allow_small_or_imprecise_dtypes=True)
            gp.iota(g.kramp[:, :], [[1, TOPK]], base=0, channel_multiplier=0, allow_small_or_imprecise_dtypes=True)
            gp.iota(g.slot_base[:, :], [[ST, E1]], base=0, channel_multiplier=0, allow_small_or_imprecise_dtypes=True)
            gp.iota(g.token_less[:, :], [[P, TT]], base=-int(NOWHERE), channel_multiplier=1,
                    allow_small_or_imprecise_dtypes=True).then_inc(step, 1)
            gp.wait_ge(step, 1)
            gp.affine_select(out=g.ident[:, :], in_=g.ident[:, :], compare_op=ALU.not_equal, fill=1.0,
                             base=0, pattern=[[-1, P]], channel_multiplier=1)
            gp.affine_select(out=g.ident_b[:, :], in_=g.ident_b[:, :], compare_op=ALU.not_equal, fill=1.0,
                             base=0, pattern=[[-1, P]], channel_multiplier=1)
            gp.affine_select(out=g.before_b[:, :], in_=g.before_b[:, :], compare_op=ALU.is_gt, fill=0.0,
                             base=0, pattern=[[1, P]], channel_multiplier=-1)
            gp.affine_select(out=g.headmask[:, :], in_=g.headmask[:, :], compare_op=ALU.is_ge, fill=0.0,
                             base=0, pattern=[[-HD, P // HD], [0, HD]], channel_multiplier=1).then_inc(step, 1)
            gp.wait_ge(step, 2)
            gp.affine_select(out=g.headmask[:, :], in_=g.headmask[:, :], compare_op=ALU.is_ge, fill=0.0,
                             base=HD - 1, pattern=[[HD, P // HD], [0, HD]], channel_multiplier=-1).then_inc(made, 1)
            gp.wait_ge(made, 1)


def semaphores(nc, ctx, stage):
    made = []

    def clear():
        nc.clear_and_free_semaphores(made)
        nc.all_engine_barrier()

    ctx.callback(clear)

    def sem(name):
        made.append(nc.alloc_semaphore(name=f"{stage}_{name}"))
        return made[-1]

    return sem


def cumulate(v, out, ones_zero, src, n, groups):
    for e in range(groups):
        last = v.tensor_tensor_scan(out[:, :, e], src[:, :, e], ones_zero[:, 0:n], 0.0, ALU.add, ALU.add)
    return last


def front(nc, g, io):
    ctx = ExitStack()
    with ctx:
        def sb(name, shape, dt):
            return ctx.enter_context(nc.sbuf_tensor(name, shape, dt))

        sem = semaphores(nc, ctx, "f")

        ctx_raw = sb("ctx_raw", [P, KD, S], fp32)
        ctx_h = sb("ctx_h", [P, KD, S], f32r)
        ctx_l = sb("ctx_l", [P, KD, S], f32r)
        wkv_raw = sb("wkv_raw", [P, KD, 2 * D], fp32)
        wkv_h = sb("wkv_h", [P, KD, 2 * D], f32r)
        wkv_l = sb("wkv_l", [P, KD, 2 * D], f32r)
        kneg = [sb(f"kneg{n}", [P, D], fp32) for n in range(2)]
        kexp = kneg
        kf = [sb(f"kf{n}", [P, D], fp32) for n in range(2)]
        k_h = sb("k_h", [P, 4, D], f32r)
        k_l = sb("k_l", [P, 4, D], f32r)
        v_h = sb("v_h", [P, 4, D], f32r)
        v_l = sb("v_l", [P, 4, D], f32r)
        summ = sb("summ", [P, 2, KD, P], fp32)
        summ_h = sb("summ_h", [P, 2 * KD * P], f32r)
        summ_l = sb("summ_l", [P, 2 * KD * P], f32r)
        wchunk = [sb(f"wchunk{n}", [P, 1024], fp32) for n in range(3)]
        wsum = sb("wsum", [P, 24], fp32)
        wtot = sb("wtot", [P, 2], fp32)
        wall = sb("wall", [P, 2], fp32)
        tok = sb("tok", [P, TT], i32)
        tokf = sb("tokf", [P, TT], fp32)
        ge = sb("ge", [P, TT, E0 - 1], fp32)
        mask = sb("mask", [P, TT, E0], fp32)
        mask_b = sb("mask_b", [P, TT, E0], bf16)
        tot = sb("tot", [P, TT, E0], fp32)
        rank = sb("rank", [P, TT, E0], fp32)
        inc = sb("inc", [P, TT, E0], fp32)
        cnt_i = sb("cnt_i", [P, E0], i32)
        ntile = sb("ntile", [P, E0], fp32)
        upto = sb("upto", [P, E0], fp32)
        base = sb("base", [P, E0], fp32)
        base_rows = sb("base_rows", [P, E0], fp32)
        tex = sb("tex", [1, 3, SORTED + AHEAD], fp32)
        posf = sb("posf", [P, TT], fp32)
        qi = sb("qi", [P, 2, TT], i32)
        qf = sb("qf", [P, 2, TT], fp32)
        hot_row = wkv_raw[:, 0:2, :].rearrange("p a (t n) -> p (a t) n", n=P)
        hot_tile = wkv_raw[:, 2, 0:TT * (SORTED + AHEAD)].rearrange("p (t n) -> p t n", t=TT)
        idxf = sb("idxf", [P, SORTED + AHEAD], fp32)

        s = {n: sem(n) for n in (
            "tok_in wkv_in wkv_hi wkv_lo mask_ready counted rank_read hot_ready sorted_ready route_step "
            "ctx_in ctx_hi ctx_lo ctx_kept ctx_raw_free ctx_used "
            "k_ready v_ready kbank_free vbank_free kneg_ready kexp_ready kf_ready k_hi k_lo v_hi v_lo "
            "kv_used bd_ready ks_ready summ_taken summ_ready summ_hi summ_lo summ_out "
            "wsum_ready wtot_ready wall_ready wscale_ready last_step").split()}
        w_in = [sem(f"w_in{n}") for n in range(3)]
        w_free = [sem(f"w_free{n}") for n in range(3)]

        kbank, vbank = g.bank[0:2], g.bank[2:4]
        bd_bank, ks_bank, route_bank, sort_bank = g.bank[4], g.bank[5], g.bank[6], g.bank[7]
        NJ = SORTED + AHEAD

        with nc.Block() as block:
            @block.sync
            def _(sp):
                sp.dma_start(tok[:, :], io["tokens"]).then_inc(s["tok_in"], 16)
                sp.dma_start(wkv_raw[:, :, :], io["wkv"]).then_inc(s["wkv_in"], 16)
                with sp.Fori(0, B) as b:
                    sp.wait_ge(s["ctx_raw_free"], b + 1)
                    sp.dma_start(ctx_raw[:, :, :], io["ctx"][:, bass.ds(b, 1), :, :].rearrange("p a k s -> p (a k) s")).then_inc(s["ctx_in"], 16)
                    for c in range(6):
                        sp.wait_ge(w_free[c % 3], at(b, 2, c // 3))
                        sp.dma_start(wchunk[c % 3][:, :], io["wffn"][:, bass.ds(b * 6144 + c * 1024, 1024)]).then_inc(w_in[c % 3], 16)

            @block.gpsimd
            def _(gp):
                gp.wait_ge(s["wtot_ready"], 1)
                gp.partition_all_reduce(wall[:, :], wtot[:, :], P, bass.bass_isa.ReduceOp.add).then_inc(s["wall_ready"], 1)

            @block.scalar
            def _(act):
                act.wait_ge(s["wkv_in"], 16)
                act.activation(wkv_h[:, :, :], wkv_raw[:, :, :], ACT.Copy).then_inc(s["wkv_hi"], 1)
                for n in range(3):
                    act.sem_inc(w_free[n], 1)
                with act.Fori(0, B) as b:
                    act.wait_ge(s["ctx_in"], (b + 1) * 16)
                    act.wait_ge(s["ctx_used"], b + 1)
                    act.wait_ge(s["ctx_kept"], b * 32 + 32)
                    act.activation(ctx_h[:, :, :], ctx_raw[:, :, :], ACT.Copy).then_inc(s["ctx_hi"], 1)
                    for part, mine, every in (("ctx_hi", ctx_h, g.ctx_h), ("ctx_lo", ctx_l, g.ctx_l)):
                        act.wait_ge(s[part], b + 1)
                        act.dma_start(f(every[:, bass.ds(b, 1), :].rearrange("p a n -> p (a n)")),
                                     f(mine[:, :, :].rearrange("p k n -> p (k n)"))).then_inc(s["ctx_kept"], 16)
                    for t in range(4):
                        for c in ((0, 1), (2, 3), (4,), (5,))[t]:
                            act.wait_ge(w_in[c % 3], at(b, 2, c // 3) * 16)
                            act.activation(wchunk[c % 3][:, :], wchunk[c % 3][:, :], ACT.Abs,
                                           accum_out=wsum[:, bass.ds(b * 6 + c, 1)]).then_inc(w_free[c % 3], 1)
                        if t == 0:
                            act.wait_ge(s["kv_used"], b + 1)
                        act.wait_ge(s["kneg_ready"], at(b, 4, t))
                        act.activation(kexp[t % 2][:, :], kneg[t % 2][:, :], ACT.Exp).then_inc(s["kexp_ready"], 1)
                        act.wait_ge(s["v_ready"], at(b, 4, t))
                        act.activation(v_h[:, t, :], vbank[t % 2][:, :], ACT.Copy).then_inc(s["v_hi"], 1)
                        act.wait_ge(s["kf_ready"], at(b, 4, t))
                        act.activation(k_h[:, t, :], kf[t % 2][:, :], ACT.Copy).then_inc(s["k_hi"], 1)
                    act.wait_ge(s["summ_ready"], b + 1)
                    act.wait_ge(s["summ_out"], b * 32 + 32)
                    act.activation(summ_h[:, :], summ[:, :, :, :].rearrange("p w k n -> p (w k n)"), ACT.Copy).then_inc(s["summ_hi"], 1)
                    for part, (ready, mine) in enumerate((("summ_hi", summ_h), ("summ_lo", summ_l))):
                        act.wait_ge(s[ready], b + 1)
                        act.dma_start(g.summ_dram[bass.ds(b, 1), part, :, :].rearrange("a p n -> (a p) n"), f(mine[:, :])).then_inc(s["summ_out"], 16)
                act.wait_ge(s["summ_out"], 32 * (B + 1))
                act.wait_ge(s["ctx_kept"], 32 * (B + 1))

            @block.tensor
            def _(pe):
                pe.wait_ge(s["mask_ready"], 1)
                m2 = mask_b[:, :, :].rearrange("p t e -> p (t e)")
                pe.matmul(route_bank[:, 0:TT * E0], g.before_b[:, :], m2, start=True, stop=True)
                pe.matmul(route_bank[:, 256:256 + TT * E0], g.ones_b[:, :], m2, start=True, stop=True).then_inc(s["counted"], 1)
                pe.wait_ge(s["hot_ready"], 1)
                for t in range(TT):
                    last = pe.matmul(sort_bank[:, 0:NJ], hot_row[:, t, :], hot_tile[:, t, :], start=(t == 0), stop=(t == TT - 1))
                last.then_inc(s["sorted_ready"], 1)
                pe.wait_ge(s["wkv_lo"], 1)
                pe.wait_ge(s["wkv_hi"], 1)
                pe.sem_inc(s["ctx_used"], 1)
                pe.sem_inc(s["kv_used"], 1)
                with pe.Fori(0, B) as b:
                    pe.wait_ge(s["ctx_hi"], b + 1)
                    pe.wait_ge(s["ctx_lo"], b + 1)
                    for t in range(4):
                        for half, bank, free, ready in ((0, kbank, "kbank_free", "k_ready"), (1, vbank, "vbank_free", "v_ready")):
                            pe.wait_ge(s[free], at(b, 4, t))
                            for k in range(KD):
                                tok_part = [x[:, k, t * P:(t + 1) * P] for x in (ctx_h, ctx_l)]
                                w_part = [x[:, k, half * D:(half + 1) * D] for x in (wkv_h, wkv_l)]
                                last = mm3(pe, bank[t % 2][:, :], tok_part, w_part, k == 0, k == KD - 1)
                            last.then_inc(s[ready], 1)
                    pe.wait_ge(s["k_lo"], at(b, 4, 3))
                    pe.wait_ge(s["v_lo"], at(b, 4, 3))
                    pe.wait_ge(s["summ_taken"], b + 1)
                    for c in range(KD):
                        for t in range(4):
                            kp = [x[:, t, c * P:(c + 1) * P] for x in (k_h, k_l)]
                            vp = [x[:, t, c * P:(c + 1) * P] for x in (v_h, v_l)]
                            last = mm3(pe, bd_bank[:, c * P:(c + 1) * P], kp, vp, t == 0, t == 3)
                    last.then_inc(s["bd_ready"], 1)
                    for c in range(KD):
                        for t in range(4):
                            pe.matmul(ks_bank[:, c * P:(c + 1) * P], k_h[:, t, c * P:(c + 1) * P], g.ones_r[:, :], start=(t == 0), stop=False)
                            last = pe.matmul(ks_bank[:, c * P:(c + 1) * P], k_l[:, t, c * P:(c + 1) * P], g.ones_r[:, :], start=False, stop=(t == 3))
                    last.then_inc(s["ks_ready"], 1)
                    pe.wait_ge(s["ks_ready"], b + 1)
                    pe.sem_inc(s["ctx_used"], 1)
                    pe.sem_inc(s["kv_used"], 1)

            @block.vector
            def _(v):
                n = [0]

                def then(ins):
                    n[0] += 1
                    ins.then_inc(s["route_step"], 1)
                    v.wait_ge(s["route_step"], n[0])

                v.wait_ge(s["tok_in"], 16)
                then(v.tensor_copy(tokf[:, :], tok[:, :]))
                for e in range(E0 - 1):
                    last = v.tensor_scalar(ge[:, :, e], tokf[:, :], float((e + 1) * PER_EXPERT), None, ALU.is_ge)
                then(last)
                v.tensor_scalar(mask[:, :, 0], ge[:, :, 0], -1.0, 1.0, ALU.mult, ALU.add)
                for e in range(1, E0 - 1):
                    v.tensor_tensor(mask[:, :, e], ge[:, :, e - 1], ge[:, :, e], ALU.subtract)
                then(v.tensor_copy(mask[:, :, E0 - 1], ge[:, :, E0 - 2]))
                v.tensor_copy(mask_b[:, :, :], mask[:, :, :]).then_inc(s["mask_ready"], 1)
                v.wait_ge(s["wkv_hi"], 1)
                v.tensor_tensor(wkv_l[:, :, :], wkv_raw[:, :, :], f(wkv_h[:, :, :]), ALU.subtract).then_inc(s["wkv_lo"], 1)
                v.wait_ge(s["counted"], 1)
                then(v.tensor_copy(tot[:, :, :], route_bank[:, 256:256 + TT * E0].rearrange("p (t e) -> p t e", e=E0)))
                then(cumulate(v, inc, g.zeros, tot, TT, E0))
                then(v.tensor_tensor(rank[:, :, :], inc[:, :, :], tot[:, :, :], ALU.subtract))
                then(v.tensor_tensor(rank[:, :, :], rank[:, :, :], route_bank[:, 0:TT * E0].rearrange("p (t e) -> p t e", e=E0), ALU.add))
                then(v.tensor_scalar(cnt_i[:, :], inc[:, TT - 1, :], float(P - 1), None, ALU.add))
                then(v.tensor_scalar(cnt_i[:, :], cnt_i[:, :], 7, None, ALU.logical_shift_right))
                then(v.tensor_copy(ntile[:, :], cnt_i[:, :]))
                then(v.tensor_tensor_scan(upto[:, :], ntile[:, :], g.zeros[:, 0:E0], 0.0, ALU.add, ALU.add))
                then(v.tensor_tensor(base[:, :], upto[:, :], ntile[:, :], ALU.subtract))
                for e in range(1, E0):
                    v.tensor_scalar(tex[:, e - 1, :], g.ramp[0:1, 0:NJ], base[0:1, e:e + 1], None, ALU.is_ge)
                then(v.tensor_scalar(base_rows[:, :], base[:, :], float(P), None, ALU.mult))
                then(v.tensor_tensor(tex[:, 0, :], tex[:, 0, :], tex[:, 1, :], ALU.add))
                v.tensor_tensor(g.tile_expert[:, :], tex[:, 0, :], tex[:, 2, :], ALU.add)
                then(v.tensor_tensor(rank[:, :, :], rank[:, :, :], base_rows[:, :].unsqueeze(1).to_broadcast([P, TT, E0]), ALU.add))
                then(v.tensor_tensor(rank[:, :, :], rank[:, :, :], mask[:, :, :], ALU.mult))
                then(v.tensor_reduce(posf[:, :], rank[:, :, :], AX.X, ALU.add))
                then(v.tensor_copy(g.pos[:, :], posf[:, :]))
                v.tensor_scalar(qi[:, 0, :], g.pos[:, :], 7, None, ALU.logical_shift_right)
                then(v.tensor_scalar(qi[:, 1, :], g.pos[:, :], P - 1, None, ALU.bitwise_and))
                then(v.tensor_copy(qf[:, :, :], qi[:, :, :]))
                v.tensor_tensor(hot_row, g.ramp[:, :].unsqueeze(1).to_broadcast([P, TT, P]), qf[:, 1, :].unsqueeze(2).to_broadcast([P, TT, P]), ALU.is_equal)
                then(v.tensor_tensor(hot_tile, g.ramp[:, 0:NJ].unsqueeze(1).to_broadcast([P, TT, NJ]), qf[:, 0, :].unsqueeze(2).to_broadcast([P, TT, NJ]), ALU.is_equal))
                v.tensor_tensor(hot_tile, hot_tile, g.token_less[:, :].unsqueeze(2).to_broadcast([P, TT, NJ]), ALU.mult).then_inc(s["hot_ready"], 1)
                v.wait_ge(s["sorted_ready"], 1)
                then(v.tensor_scalar(idxf[:, :], sort_bank[:, 0:NJ], NOWHERE, float(T - 1), ALU.add, ALU.min))
                then(v.tensor_copy(g.sorted_idx[:, :], idxf[:, :]))

                v.sem_inc(s["ctx_raw_free"], 1)
                for name in ("kbank_free", "vbank_free"):
                    v.sem_inc(s[name], 2)
                v.sem_inc(s["summ_taken"], 1)
                v.sem_inc(s["ctx_kept"], 32)
                v.sem_inc(s["summ_out"], 32)
                with v.Fori(0, B) as b:
                    v.wait_ge(s["ctx_hi"], b + 1)
                    v.tensor_tensor(ctx_l[:, :, :], ctx_raw[:, :, :], f(ctx_h[:, :, :]), ALU.subtract).then_inc(s["ctx_lo"], 1)
                    v.wait_ge(s["ctx_lo"], b + 1)
                    v.sem_inc(s["ctx_raw_free"], 1)
                    for t in range(4):
                        v.wait_ge(s["k_ready"], at(b, 4, t))
                        v.tensor_scalar(kneg[t % 2][:, :], kbank[t % 2][:, :], 0.0, None, ALU.min).then_inc(s["kneg_ready"], 1)
                        v.wait_ge(s["kexp_ready"], at(b, 4, t))
                        v.scalar_tensor_tensor(out=kf[t % 2][:, :], in0=kbank[t % 2][:, :], scalar=0.0, in1=kexp[t % 2][:, :],
                                               op0=ALU.max, op1=ALU.add).then_inc(s["kf_ready"], 1)
                        v.wait_ge(s["kf_ready"], at(b, 4, t))
                        v.sem_inc(s["kbank_free"], 1)
                        v.wait_ge(s["v_hi"], at(b, 4, t))
                        v.tensor_tensor(v_l[:, t, :], vbank[t % 2][:, :], f(v_h[:, t, :]), ALU.subtract).then_inc(s["v_lo"], 1)
                        v.wait_ge(s["v_lo"], at(b, 4, t))
                        v.sem_inc(s["vbank_free"], 1)
                        v.wait_ge(s["k_hi"], at(b, 4, t))
                        v.tensor_tensor(k_l[:, t, :], kf[t % 2][:, :], f(k_h[:, t, :]), ALU.subtract).then_inc(s["k_lo"], 1)
                    hm = g.headmask[:, :].unsqueeze(1).to_broadcast([P, KD, P])
                    v.wait_ge(s["bd_ready"], b + 1)
                    v.tensor_tensor(summ[:, 0, :, :], bd_bank[:, :].rearrange("p (k n) -> p k n", n=P), hm, ALU.mult)
                    v.wait_ge(s["ks_ready"], b + 1)
                    v.tensor_tensor(summ[:, 1, :, :], ks_bank[:, :].rearrange("p (k n) -> p k n", n=P), hm, ALU.mult).then_inc(s["summ_ready"], 1)
                    v.wait_ge(s["summ_ready"], b + 1)
                    v.sem_inc(s["summ_taken"], 1)
                    v.wait_ge(s["summ_hi"], b + 1)
                    v.tensor_tensor(summ_l[:, :], summ[:, :, :, :].rearrange("p w k n -> p (w k n)"), f(summ_h[:, :]), ALU.subtract).then_inc(s["summ_lo"], 1)
                for c in range(3):
                    v.wait_ge(w_free[c], 2 * B + 1)
                v.tensor_reduce(wtot[:, 0:1], wsum[:, 0:16], AX.X, ALU.add)
                v.tensor_reduce(wtot[:, 1:2], wsum[:, 16:24], AX.X, ALU.add).then_inc(s["wtot_ready"], 1)
                v.wait_ge(s["wall_ready"], 1)
                then(v.tensor_scalar(g.wscale[:, 0:1], wall[:, 0:1], 1.0 / (2 * HID * D), 1e-5, ALU.mult, ALU.max))
                then(v.tensor_scalar(g.wscale[:, 1:2], wall[:, 1:2], 1.0 / (HID * D), 1e-5, ALU.mult, ALU.max))
                v.tensor_scalar(g.whalf[:, 0:4:2], g.wscale[:, :], 0.5, None, ALU.mult)
                then(v.tensor_scalar(g.whalf[:, 1:4:2], g.wscale[:, :], -0.5, None, ALU.mult))


def gather_rows(gp, idx1, every, col, out, rows, step, turn, arrived, passed):
    gp.tensor_copy(idx1[:, :], every[:, bass.ds(col, 1)]).then_inc(step, 1)
    gp.wait_ge(step, turn)
    gp.sem_inc(passed, 1)
    gp.indirect_dma_start(out, None, rows, bass.IndirectOffsetOnAxis(idx1[:, 0:1], 0)).then_inc(arrived, 16)


def experts0(nc, g, io):
    ctx = ExitStack()
    with ctx:
        def sb(name, shape, dt):
            return [ctx.enter_context(nc.sbuf_tensor(f"e0_{name}{u}", shape, dt)) for u in range(2)]

        sem = semaphores(nc, ctx, "e0")

        def sem2(name):
            return [sem(f"{name}{u}") for u in range(2)]

        idx1 = sb("idx1", [P, 1], i32)
        xg = sb("xg", [P, D], fp32)
        stats = sb("stats", [P, 6], fp32)
        xn = sb("xn", [P, D], fp32)
        x_h, x_l = sb("x_h", [P, KD, P], f32r), sb("x_l", [P, KD, P], f32r)
        sil = sb("sil", [P, D], fp32)
        mid = sb("mid", [P, D], fp32)
        m_h, m_l = sb("m_h", [P, KD, P], f32r), sb("m_l", [P, KD, P], f32r)
        y = sb("y", [P, D], fp32)
        mv = ctx.enter_context(nc.sbuf_tensor("e0_mv", [P, 2, 2], fp32))
        var = ctx.enter_context(nc.sbuf_tensor("e0_var", [P, 2], fp32))
        rstd = ctx.enter_context(nc.sbuf_tensor("e0_rstd", [P, 2], fp32))
        wchunk = [ctx.enter_context(nc.sbuf_tensor(f"e0_wraw{n}", [P, 1024], fp32)) for n in range(3)]
        wneg = [ctx.enter_context(nc.sbuf_tensor(f"e0_wneg{n}", [P, 1024], bf16)) for n in range(3)]

        passed = {e: sem(f"passed_{e}") for e in ("pool", "dve")}
        idx_step, arrived, stats_step, var_ready, rstd_ready = sem2("idx_step"), sem2("arrived"), sem2("stats_step"), sem("var_ready"), sem("rstd_ready")
        mv_ready = sem("mv_ready")
        xn_ready, xT_ready, xh_ready, xl_ready = sem2("xn_ready"), sem2("xT_ready"), sem2("xh_ready"), sem2("xl_ready")
        a_ready, sil_ready, mid_ready = sem2("a_ready"), sem2("sil_ready"), sem2("mid_ready")
        mT_ready, mh_ready, ml_ready = sem2("mT_ready"), sem2("mh_ready"), sem2("ml_ready")
        y_ready, y_copied, y_out = sem2("y_ready"), sem2("y_copied"), sem2("y_out")
        w_in = [sem(f"w_in{n}") for n in range(3)]
        w_neg = [sem(f"w_neg{n}") for n in range(3)]
        w_done = [sem(f"w_done{n}") for n in range(3)]

        abank, xbank, mbank, ybank = g.bank[0:2], g.bank[2:4], g.bank[4:6], g.bank[6:8]
        PAIRS = SORTED // 2
        QTURNS = 8

        def chunk(i, c):
            return (i * 2 + c) * 1024 if c < 2 else i * 1024 + 2 * HID * KD

        with nc.Block() as block:
            @block.sync
            def _(sp):
                for u in range(2):
                    sp.sem_inc(y_out[u], 16)

                def turn(i, quantise):
                    if quantise:
                        for c in range(3):
                            sp.wait_ge(w_done[c], i + 1)
                            sp.dma_start(wchunk[c][:, :], io["wffn"][:, bass.ds(chunk(i, c), 1024)]).then_inc(w_in[c], 16)
                    for u in range(2):
                        sp.wait_ge(y_copied[u], i + 2)
                        sp.dma_start(g.sorted_y[bass.ds(i * (2 * P) + u * P, P), :], y[u][:, :]).then_inc(y_out[u], 16)

                with sp.Fori(0, QTURNS) as i:
                    turn(i, True)
                with sp.Fori(QTURNS, PAIRS) as i:
                    turn(i, False)
                for u in range(2):
                    sp.wait_ge(y_out[u], 16 * (PAIRS + 1))

            @block.gpsimd
            def _(gp):
                def fetch(n):
                    for u in range(2):
                        gather_rows(gp, idx1[u], g.sorted_idx, n * 2 + u, xg[u][:, :], io["x"], idx_step[u], n + 1, arrived[u], passed["pool"])

                def deviation(n):
                    gp.wait_ge(var_ready, n + 1)
                    gp.tensor_tensor(rstd[:, :], var[:, :], g.minus_half[:, 0:2], ALU.pow).then_inc(rstd_ready, 1)

                fetch(0)
                deviation(0)
                with gp.Fori(0, PAIRS) as i:
                    for u in range(2):
                        gp.wait_ge(xn_ready[u], i + 1)
                    fetch(i + 1)
                    deviation(i + 1)

            @block.scalar
            def _(act):
                def split_x(n):
                    for u in range(2):
                        act.wait_ge(xT_ready[u], n + 1)
                        act.activation(x_h[u][:, :, :].rearrange("p k n -> p (k n)"), xbank[u][:, :], ACT.Copy).then_inc(xh_ready[u], 1)

                for u in range(2):
                    act.sem_inc(y_copied[u], 1)
                split_x(0)
                with act.Fori(0, PAIRS) as i:
                    for u in range(2):
                        act.wait_ge(a_ready[u], i + 1)
                        act.activation(sil[u][:, :], abank[u][:, :], ACT.Silu).then_inc(sil_ready[u], 1)
                    split_x(i + 1)
                    for u in range(2):
                        act.wait_ge(mT_ready[u], i + 1)
                        act.activation(m_h[u][:, :, :].rearrange("p k n -> p (k n)"), mbank[u][:, :], ACT.Copy).then_inc(mh_ready[u], 1)
                    for u in range(2):
                        act.wait_ge(y_ready[u], i + 1)
                        act.wait_ge(y_out[u], (i + 1) * 16)
                        act.activation(y[u][:, :], ybank[u][:, :], ACT.Copy).then_inc(y_copied[u], 1)

            @block.tensor
            def _(pe):
                def turn_x(n):
                    for u in range(2):
                        pe.wait_ge(xn_ready[u], n + 1)
                        for k in range(KD):
                            last = pe.transpose(xbank[u][:, k * P:(k + 1) * P], xn[u][:, k * P:(k + 1) * P], g.ident[:, :])
                        last.then_inc(xT_ready[u], 1)

                turn_x(0)
                with pe.Fori(0, PAIRS) as i:
                    e = [pe.value_load(g.tile_expert[0:1, bass.ds(i * 2 + u, 1)], min_val=0, max_val=E0 - 1) for u in range(2)]

                    def w(u, k):
                        return [x[:, bass.ds(e[u], 1), k * S:(k + 1) * S].rearrange("p a n -> p (a n)") for x in (g.ctx_h, g.ctx_l)]

                    for u in range(2):
                        pe.wait_ge(xh_ready[u], i + 1)
                        pe.wait_ge(xl_ready[u], i + 1)
                        for k in range(KD):
                            last = mm3(pe, abank[u][:, :], (x_h[u][:, k, :], x_l[u][:, k, :]), w(u, k), k == 0, k == KD - 1)
                        last.then_inc(a_ready[u], 1)
                    turn_x(i + 1)
                    for u in range(2):
                        pe.wait_ge(mid_ready[u], i + 1)
                        for k in range(KD):
                            last = pe.transpose(mbank[u][:, k * P:(k + 1) * P], mid[u][:, k * P:(k + 1) * P], g.ident[:, :])
                        last.then_inc(mT_ready[u], 1)
                    for u in range(2):
                        pe.wait_ge(mh_ready[u], i + 1)
                        pe.wait_ge(ml_ready[u], i + 1)
                        pe.wait_ge(y_copied[u], i + 1)
                        for k in range(KD):
                            last = mm3(pe, ybank[u][:, :], (m_h[u][:, k, :], m_l[u][:, k, :]), w(u, k), k == 0, k == KD - 1)
                        last.then_inc(y_ready[u], 1)

            @block.vector
            def _(v):
                def normalise(n):
                    for u in range(2):
                        v.wait_ge(arrived[u], (n + 1) * 16)
                        v.bn_stats(stats[u][:, :], xg[u][:, :]).then_inc(stats_step[u], 1)
                    for u in range(2):
                        v.wait_ge(stats_step[u], n + 1)
                        v.sem_inc(passed["dve"], 1)
                        last = v.bn_aggr(mv[:, u, :], stats[u][:, :])
                    last.then_inc(mv_ready, 1)
                    v.wait_ge(mv_ready, n + 1)
                    v.tensor_scalar(var[:, :], mv[:, :, 1], LN_EPS, None, ALU.add).then_inc(var_ready, 1)
                    v.wait_ge(rstd_ready, n + 1)
                    for u in range(2):
                        v.tensor_scalar(xn[u][:, :], xg[u][:, :], mv[:, u, 0:1], rstd[:, u:u + 1], ALU.subtract, ALU.mult).then_inc(xn_ready[u], 1)

                def split_x(n):
                    for u in range(2):
                        v.wait_ge(xh_ready[u], n + 1)
                        v.tensor_tensor(x_l[u][:, :, :].rearrange("p k n -> p (k n)"), xbank[u][:, :],
                                        f(x_h[u][:, :, :].rearrange("p k n -> p (k n)")), ALU.subtract).then_inc(xl_ready[u], 1)

                def turn(i, quantise):
                    for u in range(2):
                        v.wait_ge(xT_ready[u], i + 1)
                    normalise(i + 1)
                    for u in range(2):
                        v.wait_ge(sil_ready[u], i + 1)
                        v.tensor_tensor(mid[u][:, :], abank[u][:, :], sil[u][:, :], ALU.mult).then_inc(mid_ready[u], 1)
                    split_x(i + 1)
                    for u in range(2):
                        v.wait_ge(mh_ready[u], i + 1)
                        v.tensor_tensor(m_l[u][:, :, :].rearrange("p k n -> p (k n)"), mbank[u][:, :],
                                        f(m_h[u][:, :, :].rearrange("p k n -> p (k n)")), ALU.subtract).then_inc(ml_ready[u], 1)
                    if quantise:
                        for c in range(3):
                            half = g.whalf[:, 2 * (c // 2):2 * (c // 2) + 1]
                            less = g.whalf[:, 2 * (c // 2) + 1:2 * (c // 2) + 2]
                            v.wait_ge(w_in[c], (i + 1) * 16)
                            v.tensor_scalar(wneg[c][:, :], wchunk[c][:, :], less, None, ALU.is_lt).then_inc(w_neg[c], 1)
                            v.wait_ge(w_neg[c], i + 1)
                            v.scalar_tensor_tensor(out=g.w3[:, bass.ds(chunk(i, c), 1024)], in0=wchunk[c][:, :], scalar=half,
                                                   in1=wneg[c][:, :], op0=ALU.is_gt, op1=ALU.subtract).then_inc(w_done[c], 1)

                for c in range(3):
                    v.sem_inc(w_done[c], 1)
                normalise(0)
                split_x(0)
                with v.Fori(0, QTURNS) as i:
                    turn(i, True)
                with v.Fori(QTURNS, PAIRS) as i:
                    turn(i, False)


def there(t, pairs):
    return not isinstance(t[0], int) or 0 <= t[0] < pairs


def ffn0(nc, g, io):
    PAIRS = TT // 2
    ctx = ExitStack()
    with ctx:
        def one(name, shape, dt):
            return ctx.enter_context(nc.sbuf_tensor(f"f0_{name}", shape, dt))

        def sb(name, shape, dt):
            return [one(f"{name}{u}", shape, dt) for u in range(2)]

        sem = semaphores(nc, ctx, "f0")

        def sem2(name):
            return [sem(f"{name}{u}") for u in range(2)]

        norm_b = one("norm_b", [P, D], fp32)
        idx1, xin, yin, xl, h = sb("idx1", [P, 1], i32), sb("xin", [P, D], fp32), sb("yin", [P, D], fp32), sb("xl", [P, D], fp32), sb("h", [P, D], fp32)
        stats, mv, var, rstd = sb("stats", [P, 6], fp32), sb("mv", [P, 2], fp32), sb("var", [P, 1], fp32), sb("rstd", [P, 1], fp32)
        ssq, msq, rms = sb("ssq", [P, 1], fp32), sb("msq", [P, 1], fp32), sb("rms", [P, 1], fp32)
        square = one("square", [P, D], fp32)
        am, qs, deq = sb("am", [P, 1], fp32), sb("qs", [P, 1], fp32), sb("deq", [P, 1], fp32)
        q, qT = sb("q", [P, D], bf16), sb("qT", [P, D], bf16)
        sg = sb("sg", [P, 512], fp32)
        h2 = sb("h2", [P, HID], fp32)
        amc = sb("amc", [P, 4], fp32)
        am2, qs2, deq2 = sb("am2", [P, 1], fp32), sb("qs2", [P, 1], fp32), sb("deq2", [P, 1], fp32)
        q2, q2T = one("q2", [P, HID], bf16), one("q2T", [P, HID], bf16)
        stats2, mv2, var2, rstd2 = sb("stats2", [P, 6], fp32), sb("mv2", [P, 2], fp32), sb("var2", [P, 1], fp32), sb("rstd2", [P, 1], fp32)
        xn = sb("xn", [P, D], fp32)

        passed = {e: sem(f"passed_{e}") for e in ("pool", "dve")}
        norm_in = sem("norm_in")
        x_in, idx_step, y_in, x1_ready = sem2("x_in"), sem2("idx_step"), sem2("y_in"), sem2("x1_ready")
        st1, st2, st3, st4, st5, st6, st7, st8 = [sem2(f"pre_step{n}") for n in range(8)]
        mt1, mt2, mt3 = [sem2(f"mid_step{n}") for n in range(3)]
        po1, po2 = [sem2(f"post_step{n}") for n in range(2)]
        var_ready, rstd_ready, xl_ready, r1_ready = sem2("var_ready"), sem2("rstd_ready"), sem2("xl_ready"), sem2("r1_ready")
        ssq_ready, msq_ready, rms_ready = sem2("ssq_ready"), sem2("msq_ready"), sem2("rms_ready")
        deq_ready, q_ready, qT_ready, qT_copied = sem2("deq_ready"), sem2("q_ready"), sem2("qT_ready"), sem2("qT_copied")
        v_ready, g_ready, sg_ready, h2_ready, amc_ready = sem("v_ready"), sem("g_ready"), sem("sg_ready"), sem("h2_ready"), sem("amc_ready")
        qs2_ready, h2_scaled, q2_ready, q2T_ready, q2T_copied = sem2("qs2_ready"), sem2("h2_scaled"), sem2("q2_ready"), sem2("q2T_ready"), sem2("q2T_copied")
        o_ready, x2_ready, var2_ready, rstd2_ready = sem2("o_ready"), sem2("x2_ready"), sem2("var2_ready"), sem2("rstd2_ready")
        xn_ready, xT_ready, xh_ready, xlo_ready = sem2("xn_ready"), sem2("xT_ready"), sem2("xh_ready"), sem2("xlo_ready")

        vbank, gbank, tbank, obank, sbank = g.bank[0:2], g.bank[2:4], [x[:, :].bitcast(bf16) for x in g.bank[4:6]], g.bank[6], g.bank[7]
        sbank_b = sbank[:, :].bitcast(bf16)
        w_out = g.w3[:, KD * 2 * HID:].rearrange("p (k n) -> p k n", n=D)

        def w_gv(k, col):
            return g.w3[:, k * 2 * HID + col:k * 2 * HID + col + 512]

        def tile(i, u, d):
            return i + (u + d) // 2, (u + d) % 2

        def seq(t, c):
            return t[0] * 8 + (4 * t[1] + c + 1)

        def turns(eng, half):
            for u in range(2):
                half(0, u)
            with eng.Fori(1, PAIRS - 1) as i:
                for u in range(2):
                    half(i, u)
            for i in (PAIRS - 1, PAIRS):
                for u in range(2):
                    half(i, u)

        def row(t):
            return t[0] * (2 * P) + t[1] * P

        with nc.Block() as block:
            @block.sync
            def _(sp):
                sp.dma_start(norm_b[:, :], io["norm_w"][0, :].partition_broadcast(P)).then_inc(norm_in, 16)

                def load(j, u):
                    sp.dma_start(xin[u][:, :], io["x"][bass.ds(row((j, u)), P), :]).then_inc(x_in[u], 16)

                load(0, 0)
                load(0, 1)
                with sp.Fori(1, PAIRS) as j:
                    for u in range(2):
                        sp.wait_ge(r1_ready[u], j)
                        load(j, u)

            @block.gpsimd
            def _(gp):
                def fetch(t):
                    j, u = t
                    if not isinstance(j, int) or j > 0:
                        gp.wait_ge(x1_ready[u], j)
                    gather_rows(gp, idx1[u], g.pos, j * 2 + u, yin[u][:, :], g.sorted_y, idx_step[u], j + 1, y_in[u], passed["pool"])

                def prepare(t):
                    j, u = t
                    gp.wait_ge(x_in[u], (j + 1) * 16)
                    gp.wait_ge(y_in[u], (j + 1) * 16)
                    gp.tensor_tensor(xin[u][:, :], xin[u][:, :], yin[u][:, :], ALU.add).then_inc(x1_ready[u], 1)
                    gp.wait_ge(var_ready[u], j + 1)
                    gp.tensor_tensor(rstd[u][:, :], var[u][:, :], g.minus_half[:, 0:1], ALU.pow).then_inc(rstd_ready[u], 1)
                    gp.wait_ge(xl_ready[u], j + 1)
                    gp.tensor_tensor(g.rows[:, bass.ds(j * 2 + u, 1), :].rearrange("p a n -> p (a n)"), xin[u][:, :], xl[u][:, :], ALU.add).then_inc(r1_ready[u], 1)
                    gp.wait_ge(msq_ready[u], j + 1)
                    gp.tensor_tensor(rms[u][:, :], msq[u][:, :], g.minus_half[:, 0:1], ALU.pow).then_inc(rms_ready[u], 1)

                for u in range(2):
                    fetch((0, u))
                for u in range(2):
                    prepare((0, u))

                def half(i, u):
                    t = tile(i, u, 2)
                    if there(t, PAIRS):
                        fetch(t)
                    w = tile(i, u, -2)
                    if there(w, PAIRS):
                        gp.wait_ge(var2_ready[w[1]], w[0] + 1)
                        gp.tensor_tensor(rstd2[w[1]][:, :], var2[w[1]][:, :], g.minus_half[:, 0:1], ALU.pow).then_inc(rstd2_ready[w[1]], 1)
                    if there(t, PAIRS):
                        prepare(t)

                turns(gp, half)

            @block.scalar
            def _(act):
                def squares(t):
                    j, u = t
                    act.wait_ge(xl_ready[u], j + 1)
                    act.activation(square[:, :], xl[u][:, :], ACT.Square, accum_out=ssq[u][:, :]).then_inc(ssq_ready[u], 1)

                def copy_qT(t):
                    j, u = t
                    act.wait_ge(qT_ready[u], j + 1)
                    act.activation(qT[u][:, :], sbank_b[:, 0:D], ACT.Copy).then_inc(qT_copied[u], 1)

                def silu(t, c):
                    act.wait_ge(deq_ready[t[1]], t[0] + 1)
                    act.wait_ge(g_ready, seq(t, c))
                    act.activation(sg[c % 2][:, :], gbank[c % 2][:, :], ACT.Silu, scale=deq[t[1]][:, 0:1]).then_inc(sg_ready, 1)

                for u in range(2):
                    squares((0, u))
                copy_qT((0, 0))

                def half(i, u):
                    me, before, last, after, later = [tile(i, u, d) for d in (0, -1, -2, 1, 2)]
                    if there(me, PAIRS):
                        silu(me, 0)
                    if there(before, PAIRS):
                        j, w = before
                        act.wait_ge(qs2_ready[w], j + 1)
                        act.activation(h2[w][:, :], h2[w][:, :], ACT.Copy, bias=MAGIC, scale=qs2[w][:, 0:1]).then_inc(h2_scaled[w], 1)
                    if there(me, PAIRS):
                        silu(me, 1)
                    if there(after, PAIRS):
                        copy_qT(after)
                    if there(me, PAIRS):
                        silu(me, 2)
                    if there(before, PAIRS):
                        act.wait_ge(q2T_ready[w], j + 1)
                        for n in range(2):
                            ins = act.activation(q2T[:, n * 1024:(n + 1) * 1024], tbank[n][:, :], ACT.Copy)
                        ins.then_inc(q2T_copied[w], 1)
                    if there(me, PAIRS):
                        silu(me, 3)
                    if there(later, PAIRS):
                        squares(later)
                    if there(last, PAIRS):
                        j, w = last
                        act.wait_ge(xT_ready[w], j + 1)
                        act.activation(g.xT_h[:, :, bass.ds(row(last), P)], sbank[:, :].rearrange("p (k n) -> p k n", n=P), ACT.Copy).then_inc(xh_ready[w], 1)

                turns(act, half)

            @block.tensor
            def _(pe):
                def turn_q(t):
                    j, u = t
                    pe.wait_ge(q_ready[u], j + 1)
                    for k in range(KD):
                        last = pe.transpose(sbank_b[:, k * P:(k + 1) * P], q[u][:, k * P:(k + 1) * P], g.ident_b[:, :])
                    last.then_inc(qT_ready[u], 1)

                turn_q((0, 0))

                def half(i, u):
                    me, before, last, after = [tile(i, u, d) for d in (0, -1, -2, 1)]

                    def expand(c):
                        if c >= 2 or not isinstance(i, int) or (i, u) != (0, 0):
                            pe.wait_ge(h2_ready, me[0] * 8 + (4 * u + c - 1))
                        for bank, col, ready in ((gbank, HID, g_ready), (vbank, 0, v_ready)):
                            for k in range(KD):
                                ins = pe.matmul(bank[c % 2][:, :], qT[u][:, k * P:(k + 1) * P], w_gv(k, col + c * 512), start=(k == 0), stop=(k == KD - 1))
                            ins.then_inc(ready, 1)

                    if there(me, PAIRS):
                        pe.wait_ge(qT_copied[u], me[0] + 1)
                        expand(0)
                        expand(1)
                        if there(after, PAIRS):
                            turn_q(after)
                        expand(2)
                    if there(before, PAIRS):
                        j, w = before
                        pe.wait_ge(q2_ready[w], j + 1)
                        for k in range(HID // P):
                            ins = pe.transpose(tbank[k // 8][:, (k % 8) * P:(k % 8 + 1) * P], q2[:, k * P:(k + 1) * P], g.ident_b[:, :])
                        ins.then_inc(q2T_ready[w], 1)
                    if there(me, PAIRS):
                        expand(3)
                    if there(last, PAIRS):
                        j, w = last
                        pe.wait_ge(xn_ready[w], j + 1)
                        if there(after, PAIRS):
                            pe.wait_ge(qT_copied[after[1]], after[0] + 1)
                        elif there(me, PAIRS):
                            pe.wait_ge(h2_ready, seq(me, 3))
                        else:
                            pe.wait_ge(xlo_ready[1 - w], j + w)
                        for k in range(KD):
                            ins = pe.transpose(sbank[:, k * P:(k + 1) * P], xn[w][:, k * P:(k + 1) * P], g.ident[:, :])
                        ins.then_inc(xT_ready[w], 1)
                    if there(before, PAIRS):
                        j, w = before
                        pe.wait_ge(q2T_copied[w], j + 1)
                        for k in range(HID // P):
                            ins = pe.matmul(obank[:, :], q2T[:, k * P:(k + 1) * P], w_out[:, k, :], start=(k == 0), stop=(k == HID // P - 1))
                        ins.then_inc(o_ready[w], 1)

                turns(pe, half)

            @block.vector
            def _(v):
                def then(ins, sems, t):
                    ins.then_inc(sems[t[1]], 1)
                    v.wait_ge(sems[t[1]], t[0] + 1)

                def statistics(t):
                    j, u = t
                    v.wait_ge(x1_ready[u], j + 1)
                    then(v.bn_stats(stats[u][:, :], xin[u][:, :]), st1, t)
                    v.sem_inc(passed["dve"], 1)
                    then(v.bn_aggr(mv[u][:, :], stats[u][:, :]), st2, t)
                    v.tensor_scalar(var[u][:, :], mv[u][:, 1:2], LN_EPS, None, ALU.add).then_inc(var_ready[u], 1)

                def normalise(t):
                    j, u = t
                    v.wait_ge(rstd_ready[u], j + 1)
                    v.tensor_scalar(xl[u][:, :], xin[u][:, :], mv[u][:, 0:1], rstd[u][:, :], ALU.subtract, ALU.mult).then_inc(xl_ready[u], 1)

                def mean_square(t):
                    j, u = t
                    v.wait_ge(ssq_ready[u], j + 1)
                    v.tensor_scalar(msq[u][:, :], ssq[u][:, :], 1.0 / D, LN_EPS, ALU.mult, ALU.add).then_inc(msq_ready[u], 1)

                def quantise(t):
                    j, u = t
                    v.wait_ge(rms_ready[u], j + 1)
                    then(v.scalar_tensor_tensor(out=h[u][:, :], in0=xl[u][:, :], scalar=rms[u][:, 0:1], in1=norm_b[:, :], op0=ALU.mult, op1=ALU.mult), st3, t)
                    then(v.tensor_reduce(am[u][:, :], h[u][:, :], AX.X, ALU.max, apply_absolute_value=True), st4, t)
                    then(v.tensor_scalar(am[u][:, :], am[u][:, :], 1e-5, None, ALU.max), st5, t)
                    if not isinstance(j, int) or j > 0:
                        v.wait_ge(sg_ready, j * 8 + (4 * u - 4))
                    v.tensor_scalar(deq[u][:, :], am[u][:, :], g.wscale[:, 0:1], 1.0 / QB, ALU.mult, ALU.mult).then_inc(deq_ready[u], 1)
                    then(v.reciprocal(qs[u][:, :], am[u][:, :]), st6, t)
                    then(v.tensor_scalar(qs[u][:, :], qs[u][:, :], QB, None, ALU.mult), st7, t)
                    then(v.tensor_scalar(h[u][:, :], h[u][:, :], qs[u][:, 0:1], MAGIC, ALU.mult, ALU.add), st8, t)
                    v.tensor_scalar(q[u][:, :], h[u][:, :], MAGIC, None, ALU.subtract).then_inc(q_ready[u], 1)

                def product(t, c):
                    w = t[1]
                    v.wait_ge(v_ready, seq(t, c))
                    v.wait_ge(sg_ready, seq(t, c))
                    chunk = h2[w][:, c * 512:(c + 1) * 512]
                    v.scalar_tensor_tensor(out=chunk, in0=vbank[c % 2][:, :], scalar=deq[w][:, 0:1],
                                           in1=sg[c % 2][:, :], op0=ALU.mult, op1=ALU.mult).then_inc(h2_ready, 1)
                    v.wait_ge(h2_ready, seq(t, c))
                    v.tensor_reduce(amc[w][:, c:c + 1], chunk, AX.X, ALU.max, apply_absolute_value=True).then_inc(amc_ready, 1)

                v.wait_ge(norm_in, 16)
                for u in range(2):
                    statistics((0, u))
                    normalise((0, u))
                    mean_square((0, u))
                    quantise((0, u))

                def half(i, u):
                    me, before, last, later = [tile(i, u, d) for d in (0, -1, -2, 2)]
                    if there(before, PAIRS):
                        j, w = before
                        v.wait_ge(amc_ready, seq(before, 3))
                        then(v.tensor_reduce(am2[w][:, :], amc[w][:, :], AX.X, ALU.max), mt1, before)
                        then(v.tensor_scalar(am2[w][:, :], am2[w][:, :], 1e-5, None, ALU.max), mt2, before)
                        v.tensor_scalar(deq2[w][:, :], am2[w][:, :], g.wscale[:, 1:2], 1.0 / QB, ALU.mult, ALU.mult)
                        then(v.reciprocal(qs2[w][:, :], am2[w][:, :]), mt3, before)
                        v.tensor_scalar(qs2[w][:, :], qs2[w][:, :], QB, None, ALU.mult).then_inc(qs2_ready[w], 1)
                    if there(me, PAIRS):
                        product(me, 0)
                    if there(last, PAIRS):
                        j, w = last
                        rows = g.rows[:, bass.ds(j * 2 + w, 1), :].rearrange("p a n -> p (a n)")
                        v.wait_ge(o_ready[w], j + 1)
                        v.wait_ge(r1_ready[w], j + 1)
                        then(v.scalar_tensor_tensor(out=rows, in0=obank[:, :], scalar=deq2[w][:, 0:1], in1=rows, op0=ALU.mult, op1=ALU.add), x2_ready, last)
                        v.sem_inc(passed["dve"], 1)
                        then(v.bn_stats(stats2[w][:, :], rows), po1, last)
                        v.sem_inc(passed["dve"], 1)
                        then(v.bn_aggr(mv2[w][:, :], stats2[w][:, :]), po2, last)
                        v.tensor_scalar(var2[w][:, :], mv2[w][:, 1:2], LN_EPS, None, ALU.add).then_inc(var2_ready[w], 1)
                    if there(me, PAIRS):
                        product(me, 1)
                    if there(last, PAIRS):
                        v.wait_ge(rstd2_ready[w], j + 1)
                        v.tensor_scalar(xn[w][:, :], rows, mv2[w][:, 0:1], rstd2[w][:, :], ALU.subtract, ALU.mult).then_inc(xn_ready[w], 1)
                    if there(before, PAIRS):
                        j, w = before
                        v.wait_ge(h2_scaled[w], j + 1)
                        v.tensor_scalar(q2[:, :], h2[w][:, :], MAGIC, None, ALU.subtract).then_inc(q2_ready[w], 1)
                    if there(later, PAIRS):
                        statistics(later)
                    if there(me, PAIRS):
                        product(me, 2)
                    if there(later, PAIRS):
                        normalise(later)
                    if there(me, PAIRS):
                        product(me, 3)
                    if there(later, PAIRS):
                        mean_square(later)
                    if there(last, PAIRS):
                        v.wait_ge(xh_ready[last[1]], last[0] + 1)
                        v.tensor_tensor(g.xT_l[:, :, bass.ds(row(last), P)], sbank[:, :].rearrange("p (k n) -> p k n", n=P),
                                        f(g.xT_h[:, :, bass.ds(row(last), P)]), ALU.subtract).then_inc(xlo_ready[last[1]], 1)
                    if there(later, PAIRS):
                        quantise(later)

                turns(v, half)


def attention1(nc, g, io):
    ctx = ExitStack()
    with ctx:
        def one(name, shape, dt):
            return ctx.enter_context(nc.sbuf_tensor(f"a1_{name}", shape, dt))

        def sb(name, shape, dt):
            return [one(f"{name}{u}", shape, dt) for u in range(2)]

        sem = semaphores(nc, ctx, "a1")

        def sem2(name):
            return [sem(f"{name}{u}") for u in range(2)]

        work = one("work", [P, 4 * D], fp32)
        work2 = one("work2", [P, 4 * D], fp32)
        raw = [one("raw", [P, KD * D], fp32), work2, work]
        eg = [work[:, u * D:(u + 1) * D] for u in range(2)]
        den = work[:, 2 * D:3 * D]
        att = work[:, 3 * D:4 * D]
        wq, wg, wo = [(one(n + "_h", [P, KD, D], f32r), one(n + "_l", [P, KD, D], f32r)) for n in ("wq", "wg", "wo")]
        r_raw, r_h, r_l = one("r_raw", [P, KD, E1], fp32), one("r_h", [P, KD, P], f32r), one("r_l", [P, KD, P], f32r)
        bg, nbg = one("bg", [P, KD], fp32), one("nbg", [P, KD], fp32)
        summ = one("summ_h", [P, 2 * KD * P], f32r), one("summ_l", [P, 2 * KD * P], f32r)
        qf = [work2[:, u * D:(u + 1) * D] for u in range(2)]
        qs = one("q_h", [P, D], f32r), one("q_l", [P, D], f32r)
        at_s = one("at_h", [P, KD, D], f32r), one("at_l", [P, KD, D], f32r)
        xn = [work2[:, (2 + u) * D:(3 + u) * D] for u in range(2)]
        stats, mv = one("stats", [P, 6], fp32), one("mv", [P, 2], fp32)
        var, rstd = one("var", [P, 1], fp32), one("rstd", [P, 1], fp32)
        sT = one("sT", [E1, D], fp32)

        raw_in, raw_hi, raw_lo, small_in, zeroed = [sem(f"raw_in{n}") for n in range(3)], sem("raw_hi"), sem("raw_lo"), sem("small_in"), sem("zeroed")
        r_hi, r_lo, nbg_ready = sem("r_hi"), sem("r_lo"), sem("nbg_ready")
        summ_in, q_ready, gate_ready, num_ready, den_ready = sem("summ_in"), sem("q_ready"), sem("gate_ready"), sem("num_ready"), sem("den_ready")
        neg_ready, exp_ready, qf_ready, q_hi, q_lo = sem("neg_ready"), sem("exp_ready"), sem("qf_ready"), sem("q_hi"), sem("q_lo")
        eg_ready, eg1_ready, den_full, den_inv, at_ready, at_hi, at_lo = [sem(n) for n in "eg_ready eg1_ready den_full den_inv at_ready at_hi at_lo".split()]
        o_ready, x3_ready, stats_ready, mv_ready, var_ready, rstd_ready = [sem(n) for n in "o_ready x3_ready stats_ready mv_ready var_ready rstd_ready".split()]
        xn_ready, xn_out = sem2("xn_ready"), sem2("xn_out")
        xT_ready, xhi, xlo, sc_ready, sT_ready, lg_ready, lg_copied = [sem(n) for n in "xT_ready xhi xlo sc_ready sT_ready lg_ready lg_copied".split()]
        passed = {e: sem(f"passed_{e}") for e in ("dve", "pe")}
        x3_out = sem("x3_out")

        qbank, gbank, nbank, dbank, xbank = g.bank[0:2], g.bank[2:4], [g.bank[4], g.bank[6]], g.bank[5], g.bank[7]
        obank = [g.bank[6], g.bank[4]]
        lbank = g.bank[6]

        def batches(eng, batch):
            with eng.Fori(0, B - 1) as b:
                batch(b, True)
            batch(B - 1, False)

        with nc.Block() as block:
            @block.sync
            def _(sp):
                sp.dma_start(bg[:, :], io["bg"]).then_inc(small_in, 16)
                sp.dma_start(r_raw[:, :, :], io["router"]).then_inc(small_in, 16)
                for n, w in enumerate((io["wq"], io["wg"], io["wo"])):
                    sp.dma_start(raw[n][:, :], w.rearrange("p k n -> p (k n)")).then_inc(raw_in[n], 16)
                for u in range(2):
                    sp.sem_inc(xn_out[u], 16)

                def summaries(b):
                    for part in range(2):
                        sp.dma_start(f(summ[part][:, :]), g.summ_dram[bass.ds(b, 1), part, :, :].rearrange("a p n -> (a p) n")).then_inc(summ_in, 16)

                def store(b):
                    for t in range(4):
                        sp.wait_ge(xn_ready[t % 2], at(b, 2, t // 2))
                        sp.dma_start(g.xn_dram[bass.ds(b * S + t * P, P), :], xn[t % 2][:, :]).then_inc(xn_out[t % 2], 16)

                summaries(0)
                store(0)
                with sp.Fori(1, B) as b:
                    sp.wait_ge(den_ready, b * 4)
                    summaries(b)
                    store(b)
                for u in range(2):
                    sp.wait_ge(xn_out[u], 16 * (2 * B + 1))

            @block.gpsimd
            def _(gp):
                gp.memset(f(r_h[:, :, :]), 0.0)
                gp.memset(f(r_l[:, :, :]), 0.0).then_inc(zeroed, 1)

                def low(c, b):
                    gp.wait_ge(q_hi, at(b, 4, c))
                    gp.tensor_tensor(qs[1][:, :], qf[c % 2][:, :], f(qs[0][:, :]), ALU.subtract).then_inc(q_lo, 1)

                def batch(b, more):
                    for c in range(KD):
                        gp.wait_ge(eg_ready, at(b, 4, c))
                        gp.tensor_tensor(eg[c % 2], eg[c % 2], f(g.ones_r[:, 0:1]).to_broadcast([P, D]), ALU.add).then_inc(eg1_ready, 1)
                        if c + 1 < KD:
                            low(c + 1, b)
                        gp.wait_ge(at_hi, at(b, 4, c))
                        gp.tensor_tensor(at_s[1][:, c, :], att, f(at_s[0][:, c, :]), ALU.subtract).then_inc(at_lo, 1)
                    for t in range(4):
                        gp.wait_ge(var_ready, at(b, 4, t))
                        gp.tensor_tensor(rstd[:, :], var[:, :], g.minus_half[:, 0:1], ALU.pow).then_inc(rstd_ready, 1)
                    if more:
                        low(0, b + 1)

                low(0, 0)
                batches(gp, batch)

            @block.scalar
            def _(act):
                act.wait_ge(small_in, 32)
                act.wait_ge(zeroed, 1)
                act.activation(r_h[:, :, 0:E1], r_raw[:, :, :], ACT.Copy).then_inc(r_hi, 1)
                act.activation(nbg[:, :], bg[:, :], ACT.Copy, scale=-1.0).then_inc(nbg_ready, 1)
                act.wait_ge(nbg_ready, 1)
                for n, w in enumerate((wq, wg, wo)):
                    act.wait_ge(raw_in[n], 16)
                    act.activation(w[0][:, :, :].rearrange("p k n -> p (k n)"), raw[n][:, :], ACT.Copy).then_inc(raw_hi, 1)

                def phi(c, b):
                    act.wait_ge(neg_ready, at(b, 4, c))
                    act.activation(qf[c % 2][:, :], qf[c % 2][:, :], ACT.Exp).then_inc(exp_ready, 1)

                def split(c, b):
                    act.wait_ge(qf_ready, at(b, 4, c))
                    if c:
                        act.wait_ge(den_ready, at(b, 4, c - 1))
                    act.activation(qs[0][:, :], qf[c % 2][:, :], ACT.Copy).then_inc(q_hi, 1)

                def batch(b, more):
                    for c in range(KD):
                        act.wait_ge(gate_ready, at(b, 4, c))
                        act.activation(eg[c % 2], gbank[c % 2][:, :], ACT.Exp, bias=nbg[:, c:c + 1], scale=-1.0).then_inc(eg_ready, 1)
                        if c + 1 < KD:
                            phi(c + 1, b)
                            split(c + 1, b)
                        act.wait_ge(at_ready, at(b, 4, c))
                        act.activation(at_s[0][:, c, :], att, ACT.Copy).then_inc(at_hi, 1)
                    for t in range(4):
                        if t == 2 and more:
                            phi(0, b + 1)
                            split(0, b + 1)
                        act.wait_ge(xT_ready, at(b, 4, t))
                        act.activation(g.xT_h[:, :, bass.ds(b * S + t * P, P)], xbank[:, :].rearrange("p (k n) -> p k n", n=P), ACT.Copy).then_inc(xhi, 1)
                        act.dma_start(g.x3_dram[bass.ds(b * S + t * P, P), :], g.rows[:, bass.ds(b * 4 + t, 1), :].rearrange("p a n -> p (a n)")).then_inc(x3_out, 16)
                    act.wait_ge(sc_ready, b + 1)
                    act.activation(sT[:, :], dbank[0:E1, :], ACT.Copy).then_inc(sT_ready, 1)
                    act.wait_ge(lg_ready, b + 1)
                    act.activation(g.logits[:, bass.ds(b * 4, 4), :].rearrange("p a n -> p (a n)"), lbank[:, 0:4 * E1], ACT.Copy).then_inc(lg_copied, 1)

                phi(0, 0)
                split(0, 0)
                batches(act, batch)
                act.wait_ge(x3_out, 16 * TT)

            @block.tensor
            def _(pe):
                def xT(k, b):
                    return [x[:, k, bass.ds(b * S, S)] for x in (g.xT_h, g.xT_l)]

                def project(bank, w, c, b, ready):
                    for k in range(KD):
                        last = mm3(pe, bank[:, :], [x[:, k, c * P:(c + 1) * P] for x in w], xT(k, b), k == 0, k == KD - 1)
                    last.then_inc(ready, 1)

                def query(c, b):
                    project(qbank[c % 2], wq, c, b, q_ready)

                def gate(c, b):
                    project(gbank[c % 2], wg, c, b, gate_ready)

                def batch(b, more):
                    pe.wait_ge(summ_in, (b + 1) * 32)
                    for c in range(KD):
                        if c >= 2:
                            gate(c, b)
                        if 1 <= c < KD - 1:
                            query(c + 1, b)
                        pe.wait_ge(q_lo, at(b, 4, c))
                        if c:
                            pe.wait_ge(den_full, at(b, 4, c - 1))
                        if c >= 2:
                            pe.wait_ge(at_ready, at(b, 4, c - 2))
                        for n, (bank, ready) in enumerate(((nbank[c % 2], num_ready), (dbank, den_ready))):
                            col = (n * KD + c) * P
                            mm3(pe, bank[:, :], [x[:, col:col + P] for x in summ], [x[:, :] for x in qs], True, True).then_inc(ready, 1)
                    if more:
                        query(0, b + 1)
                        gate(0, b + 1)

                    def turn(t):
                        pe.wait_ge(xn_ready[t % 2], at(b, 2, t // 2))
                        if t:
                            pe.wait_ge(xlo, at(b, 4, t - 1))
                        for k in range(KD):
                            last = pe.transpose(xbank[:, k * P:(k + 1) * P], xn[t % 2][:, k * P:(k + 1) * P], g.ident[:, :])
                        last.then_inc(xT_ready, 1)

                    for t in range(4):
                        if t == 0:
                            pe.wait_ge(at_hi, at(b, 4, 3))
                            pe.wait_ge(at_lo, at(b, 4, 3))
                        if t >= 2:
                            turn(t - 2)
                        for c in range(KD):
                            last = mm3(pe, obank[t % 2][:, :], [x[:, c, t * P:(t + 1) * P] for x in at_s], [x[:, c, :] for x in wo], c == 0, c == KD - 1)
                        last.then_inc(o_ready, 1)
                    turn(2)
                    if more:
                        query(1, b + 1)
                    turn(3)
                    if more:
                        gate(1, b + 1)
                    pe.wait_ge(xlo, at(b, 4, 3))
                    for k in range(KD):
                        last = mm3(pe, dbank[:, :], [x[:, k, :] for x in (r_h, r_l)], xT(k, b), k == 0, k == KD - 1)
                    last.then_inc(sc_ready, 1)
                    pe.wait_ge(sT_ready, b + 1)
                    pe.sem_inc(passed["pe"], 1)
                    for t in range(4):
                        last = pe.transpose(lbank[:, t * E1:(t + 1) * E1], sT[:, t * P:(t + 1) * P], g.ident[0:E1, 0:E1])
                    last.then_inc(lg_ready, 1)

                pe.wait_ge(raw_lo, 1)
                query(0, 0)
                query(1, 0)
                pe.wait_ge(raw_lo, 2)
                gate(0, 0)
                gate(1, 0)
                pe.wait_ge(raw_lo, 3)
                pe.wait_ge(r_lo, 1)
                batches(pe, batch)

            @block.vector
            def _(v):
                v.wait_ge(r_hi, 1)
                v.tensor_tensor(r_l[:, :, 0:E1], r_raw[:, :, :], f(r_h[:, :, 0:E1]), ALU.subtract).then_inc(r_lo, 1)
                for n, w in enumerate((wq, wg, wo)):
                    v.wait_ge(raw_hi, n + 1)
                    v.tensor_tensor(w[1][:, :, :].rearrange("p k n -> p (k n)"), raw[n][:, :], f(w[0][:, :, :].rearrange("p k n -> p (k n)")), ALU.subtract).then_inc(raw_lo, 1)

                def negative(c, b):
                    v.wait_ge(q_ready, at(b, 4, c))
                    v.tensor_scalar(qf[c % 2][:, :], qbank[c % 2][:, :], 0.0, None, ALU.min).then_inc(neg_ready, 1)

                def phi(c, b):
                    v.wait_ge(exp_ready, at(b, 4, c))
                    v.scalar_tensor_tensor(out=qf[c % 2][:, :], in0=qbank[c % 2][:, :], scalar=0.0, in1=qf[c % 2][:, :],
                                           op0=ALU.max, op1=ALU.add).then_inc(qf_ready, 1)

                def batch(b, more):
                    for c in range(KD):
                        if c + 1 < KD:
                            negative(c + 1, b)
                        v.wait_ge(eg1_ready, at(b, 4, c))
                        v.wait_ge(den_ready, at(b, 4, c))
                        v.scalar_tensor_tensor(out=den, in0=dbank[:, :], scalar=ATT_EPS, in1=eg[c % 2], op0=ALU.add, op1=ALU.mult).then_inc(den_full, 1)
                        if c + 1 < KD:
                            phi(c + 1, b)
                        v.wait_ge(den_full, at(b, 4, c))
                        v.reciprocal(den, den).then_inc(den_inv, 1)
                        v.wait_ge(den_inv, at(b, 4, c))
                        if c:
                            v.wait_ge(at_lo, at(b, 4, c - 1))
                        v.tensor_tensor(att, nbank[c % 2][:, :], den, ALU.mult).then_inc(at_ready, 1)

                    def normalise(t):
                        n = at(b, 4, t)
                        rows = g.rows[:, bass.ds(b * 4 + t, 1), :].rearrange("p a n -> p (a n)")
                        v.wait_ge(o_ready, n)
                        v.tensor_tensor(rows, obank[t % 2][:, :], rows, ALU.add).then_inc(x3_ready, 1)
                        v.wait_ge(x3_ready, n)
                        v.sem_inc(passed["dve"], 1)
                        v.bn_stats(stats[:, :], rows).then_inc(stats_ready, 1)
                        v.wait_ge(stats_ready, n)
                        v.sem_inc(passed["dve"], 1)
                        v.bn_aggr(mv[:, :], stats[:, :]).then_inc(mv_ready, 1)
                        v.wait_ge(mv_ready, n)
                        v.tensor_scalar(var[:, :], mv[:, 1:2], LN_EPS, None, ALU.add).then_inc(var_ready, 1)
                        v.wait_ge(rstd_ready, n)
                        v.wait_ge(xn_out[t % 2], at(b, 2, t // 2) * 16)
                        v.tensor_scalar(xn[t % 2][:, :], rows, mv[:, 0:1], rstd[:, :], ALU.subtract, ALU.mult).then_inc(xn_ready[t % 2], 1)

                    def split(t):
                        v.wait_ge(xhi, at(b, 4, t))
                        v.tensor_tensor(g.xT_l[:, :, bass.ds(b * S + t * P, P)], xbank[:, :].rearrange("p (k n) -> p k n", n=P),
                                        f(g.xT_h[:, :, bass.ds(b * S + t * P, P)]), ALU.subtract).then_inc(xlo, 1)

                    normalise(0)
                    normalise(1)
                    for t in range(2, 4):
                        split(t - 2)
                        normalise(t)
                    if more:
                        negative(0, b + 1)
                        phi(0, b + 1)
                    split(2)
                    split(3)

                v.wait_ge(raw_lo, 3)
                negative(0, 0)
                phi(0, 0)
                batches(v, batch)


def route1(nc, g, io):
    ctx = ExitStack()
    with ctx:
        def sb(name, shape, dt=fp32):
            return ctx.enter_context(nc.sbuf_tensor(f"r1_{name}", shape, dt))

        sem = semaphores(nc, ctx, "r1")
        top, prob, mask = sb("top", [P, TT]), sb("prob", [P, TT, E1]), sb("mask", [P, TT, E1])
        m8 = sb("m8", [P, TT, 8])
        eq, cum = sb("eq", [P, TT, E1]), sb("cum", [P, TT, E1])
        ngt, wsum = sb("ngt", [P, TT]), sb("wsum", [P, TT])
        mask_b = sb("mask_b", [P, TT, E1], bf16)
        order, wn, tot, inc = sb("order", [P, TT, E1]), sb("wn", [P, TT, E1]), sb("tot", [P, TT, E1]), sb("inc", [P, TT, E1])
        high, ok, row, tile = sb("high", [P, TT, E1]), sb("ok", [P, TT, E1]), sb("row", [P, TT, E1]), sb("tile", [P, TT, E1])
        pick, prod = sb("pick", [P, TT, TOPK, E1]), sb("prod", [P, TT, TOPK, E1])
        krow, ktile, kw = sb("krow", [P, TT, TOPK]), sb("ktile", [P, TT, TOPK]), sb("kw", [P, TT, TOPK])
        hot_row = sb("hot_row", [P, TT * TOPK, P], bf16)
        hot_tile = sb("hot_tile", [P, TT * TOPK, 5, SLOTS], bf16)
        kparts = sb("kparts", [P, 5, TT * TOPK], bf16)
        rest = sb("rest", [P, 3, TT * TOPK])
        summed = sb("summed", [P, 5, SLOTS])
        found = sb("found", [P, 3, SLOTS])
        ktok = sb("ktok", [P, TT * TOPK])
        step, exp_ready, mask_ready, counted, hot_ready, slots_ready, shifted = [sem(n) for n in "step exp_ready mask_ready counted hot_ready slots_ready shifted".split()]
        raw_in = [sem(f"raw_in{n}") for n in range(2)]
        raw_hi, raw_lo, zeroed = sem("raw_hi"), sem("raw_lo"), sem("zeroed")
        cbank, sbank = g.bank[0], g.bank[1]

        def place(n):
            parts, k, width = pieces[n][1][0].shape
            return raw[n % 2][0:parts, 0:k * width].rearrange("p (k n) -> p k n", k=k)

        F = SFT * P
        wg, wu, wd = g.shared_w

        raw = sb("raw0", [P, SFF]), sb("raw1", [P, SFF])

        def piece(src, parts, k0, k1, width, w):
            return src, [x[0:parts, k0:k1, 0:width] for x in w]

        pieces = [piece(io["sw_gate"][:, k:k + 1, :], P, k, k + 1, SFF, wg) for k in range(KD)]
        pieces += [piece(io["sw_up"][:, k:k + 1, :], P, k, k + 1, SFF, wu) for k in range(KD)]
        down = io["sw_down"][0:5 * P, :].rearrange("(k p) n -> p k n", p=P)
        pieces += [piece(down[:, k:k + 1, :], P, k, k + 1, D, wd) for k in range(SFT - 1)]
        pieces.append(piece(io["sw_down"][5 * P:SFF, :].rearrange("(a p) n -> p a n", a=1), SLAST, 5, 6, D, wd))

        def over(ap, n=E1):
            return ap.unsqueeze(len(ap.shape)).to_broadcast(list(ap.shape) + [n])

        with nc.Block() as block:
            @block.sync
            def _(sp):
                for n, (src, parts) in enumerate(pieces):
                    if n >= 2:
                        sp.wait_ge(raw_lo, n - 1)
                    sp.dma_start(place(n), src).then_inc(raw_in[n % 2], 16)

            @block.gpsimd
            def _(gp):
                for w in (*wg, *wu):
                    last = gp.memset(f(w[:, :, SFF:F]), 0.0)
                last.then_inc(zeroed, 1)
                gp.wait_ge(zeroed, 1)
                for w in wd:
                    last = gp.memset(f(w[SLAST:P, SFT - 1, :]), 0.0)
                last.then_inc(zeroed, 1)
                gp.wait_ge(zeroed, 2)
                for n, (_, parts) in enumerate(pieces):
                    if n == len(pieces) - 1:
                        gp.wait_ge(raw_lo, n)
                    gp.wait_ge(raw_hi, n + 1)
                    gp.tensor_tensor(parts[1][:, 0, :], place(n)[:, 0, :], f(parts[0][:, 0, :]), ALU.subtract).then_inc(raw_lo, 1)
                gp.wait_ge(raw_lo, len(pieces))

            @block.scalar
            def _(act):
                act.wait_ge(shifted, 1)
                act.activation(prob[:, :, :], prob[:, :, :], ACT.Exp).then_inc(exp_ready, 1)
                for n, (_, parts) in enumerate(pieces):
                    act.wait_ge(raw_in[n % 2], 16 * (n // 2 + 1))
                    act.activation(parts[0], place(n), ACT.Copy).then_inc(raw_hi, 1)

            @block.tensor
            def _(pe):
                pe.wait_ge(mask_ready, 1)
                m2 = mask_b[:, :, :].rearrange("p t e -> p (t e)")
                pe.matmul(cbank[:, 0:256], g.before_b[:, :], m2, start=True, stop=True)
                pe.matmul(cbank[:, 256:512], g.ones_b[:, :], m2, start=True, stop=True).then_inc(counted, 1)
                pe.wait_ge(hot_ready, 1)
                for n in range(TT * TOPK):
                    last = pe.matmul(sbank[:, 0:5 * SLOTS], hot_row[:, n, :], hot_tile[:, n, :, :].rearrange("p a n -> p (a n)"),
                                     start=(n == 0), stop=(n == TT * TOPK - 1))
                last.then_inc(slots_ready, 1)

            @block.vector
            def _(v):
                n = [0]

                def then(ins):
                    n[0] += 1
                    ins.then_inc(step, 1)
                    v.wait_ge(step, n[0])

                then(v.tensor_reduce(top[:, :], g.logits[:, :, :], AX.X, ALU.max))
                v.tensor_tensor(prob[:, :, :], g.logits[:, :, :], over(top[:, :]), ALU.subtract).then_inc(shifted, 1)
                v.wait_ge(exp_ready, 1)
                then(v.tensor_reduce(wsum[:, :], prob[:, :, :], AX.X, ALU.add))
                then(v.reciprocal(wsum[:, :], wsum[:, :]))
                then(v.tensor_tensor(prob[:, :, :], prob[:, :, :], over(wsum[:, :]), ALU.mult))
                for t in range(TT):
                    last = v.max(m8[:, t, :], prob[:, t, :])
                then(last)
                v.tensor_tensor(mask[:, :, :], prob[:, :, :], over(m8[:, :, TOPK - 1]), ALU.is_gt)
                then(v.tensor_tensor(eq[:, :, :], prob[:, :, :], over(m8[:, :, TOPK - 1]), ALU.is_equal))
                v.tensor_reduce(ngt[:, :], mask[:, :, :], AX.X, ALU.add)
                for t in range(TT):
                    last = v.tensor_tensor_scan(cum[:, t, :], eq[:, t, :], g.zeros[:, 0:E1], 0.0, ALU.add, ALU.add)
                then(last)
                then(v.tensor_tensor(cum[:, :, :], cum[:, :, :], over(ngt[:, :]), ALU.add))
                then(v.tensor_scalar(cum[:, :, :], cum[:, :, :], float(TOPK), None, ALU.is_le))
                then(v.tensor_tensor(eq[:, :, :], eq[:, :, :], cum[:, :, :], ALU.mult))
                then(v.tensor_tensor(mask[:, :, :], mask[:, :, :], eq[:, :, :], ALU.add))
                v.tensor_copy(mask_b[:, :, :], mask[:, :, :]).then_inc(mask_ready, 1)
                then(v.tensor_tensor(wn[:, :, :], prob[:, :, :], mask[:, :, :], ALU.mult))
                then(v.tensor_reduce(wsum[:, :], wn[:, :, :], AX.X, ALU.add))
                then(v.tensor_scalar(wsum[:, :], wsum[:, :], 1e-20, None, ALU.add))
                then(v.reciprocal(wsum[:, :], wsum[:, :]))
                then(v.tensor_tensor(wn[:, :, :], wn[:, :, :], over(wsum[:, :]), ALU.mult))
                for t in range(TT):
                    last = v.tensor_tensor_scan(order[:, t, :], mask[:, t, :], g.zeros[:, 0:E1], 0.0, ALU.add, ALU.add)
                then(last)
                then(v.tensor_tensor(order[:, :, :], order[:, :, :], mask[:, :, :], ALU.subtract))
                v.wait_ge(counted, 1)
                then(v.tensor_copy(tot[:, :, :], cbank[:, 256:512].rearrange("p (t e) -> p t e", e=E1)))
                then(cumulate(v, inc, g.zeros, tot, TT, E1))
                then(v.tensor_tensor(inc[:, :, :], inc[:, :, :], tot[:, :, :], ALU.subtract))
                then(v.tensor_tensor(inc[:, :, :], inc[:, :, :], cbank[:, 0:256].rearrange("p (t e) -> p t e", e=E1), ALU.add))
                then(v.tensor_scalar(high[:, :, :], inc[:, :, :], float(P), None, ALU.is_ge))
                then(v.tensor_scalar(ok[:, :, :], inc[:, :, :], float(CAP), None, ALU.is_lt))
                then(v.scalar_tensor_tensor(out=row[:, :, :], in0=high[:, :, :], scalar=-float(P), in1=inc[:, :, :], op0=ALU.mult, op1=ALU.add))
                then(v.tensor_tensor(tile[:, :, :], high[:, :, :], g.slot_base[:, :].unsqueeze(1).to_broadcast([P, TT, E1]), ALU.add))
                then(v.tensor_scalar(tile[:, :, :], tile[:, :, :], float(SLOTS), None, ALU.subtract))
                then(v.tensor_tensor(tile[:, :, :], tile[:, :, :], ok[:, :, :], ALU.mult))
                then(v.tensor_scalar(tile[:, :, :], tile[:, :, :], float(SLOTS), None, ALU.add))
                def four(ap):
                    return ap.unsqueeze(2).to_broadcast([P, TT, TOPK, E1])
                for k in range(TOPK):
                    last = v.tensor_scalar(pick[:, :, k, :], order[:, :, :], float(k), None, ALU.is_equal)
                then(last)
                then(v.tensor_tensor(pick[:, :, :, :], pick[:, :, :, :], four(mask[:, :, :]), ALU.mult))
                for src, out in ((row, krow), (tile, ktile), (wn, kw)):
                    then(v.tensor_tensor(prod[:, :, :, :], pick[:, :, :, :], four(src[:, :, :]), ALU.mult))
                    then(v.tensor_reduce(out[:, :, :], prod[:, :, :, :], AX.X, ALU.add))
                flat = [x[:, :, :].rearrange("p t k -> p (t k)") for x in (krow, ktile, kw)]
                N = TT * TOPK
                v.tensor_tensor(hot_row[:, :, :], g.ramp[:, :].unsqueeze(1).to_broadcast([P, N, P]), over(flat[0], P), ALU.is_equal)
                for k in range(TOPK):
                    last = v.tensor_copy(ktok[:, k:N:TOPK], g.token_less[:, :])
                then(last)
                v.tensor_tensor(hot_tile[:, :, 0, :], g.ramp[:, 0:SLOTS].unsqueeze(1).to_broadcast([P, N, SLOTS]), over(flat[1], SLOTS), ALU.is_equal)
                v.tensor_copy(kparts[:, 0, :], ktok[:, :])
                then(v.tensor_copy(kparts[:, 2, :], flat[2]))
                v.tensor_tensor(rest[:, 0, :], ktok[:, :], kparts[:, 0, :], ALU.subtract)
                then(v.tensor_tensor(rest[:, 1, :], flat[2], kparts[:, 2, :], ALU.subtract))
                v.tensor_copy(kparts[:, 1, :], rest[:, 0, :])
                then(v.tensor_copy(kparts[:, 3, :], rest[:, 1, :]))
                then(v.tensor_tensor(rest[:, 2, :], rest[:, 1, :], kparts[:, 3, :], ALU.subtract))
                then(v.tensor_copy(kparts[:, 4, :], rest[:, 2, :]))
                for n_part in (1, 2, 3, 4, 0):
                    last = v.tensor_tensor(hot_tile[:, :, n_part, :], hot_tile[:, :, 0, :], over(kparts[:, n_part, :], SLOTS), ALU.mult)
                last.then_inc(hot_ready, 1)
                v.wait_ge(slots_ready, 1)
                then(v.tensor_copy(summed[:, :, :], sbank[:, 0:5 * SLOTS].rearrange("p (a n) -> p a n", n=SLOTS)))
                v.tensor_tensor(summed[:, 0, :], summed[:, 0, :], summed[:, 1, :], ALU.add)
                then(v.tensor_tensor(summed[:, 3, :], summed[:, 3, :], summed[:, 4, :], ALU.add))
                v.tensor_tensor(g.slot_weight[:, :], summed[:, 2, :], summed[:, 3, :], ALU.add)
                then(v.tensor_scalar(found[:, 0, :], summed[:, 0, :], NOWHERE, None, ALU.add))
                then(v.tensor_scalar(found[:, 1, :], found[:, 0, :], float(T - 1), None, ALU.min))
                then(v.tensor_scalar(found[:, 2, :], found[:, 0, :], g.spare[:, 0:1], None, ALU.min))
                v.tensor_copy(g.scatter_idx[:, :], found[:, 2, :])
                then(v.tensor_copy(g.gather_idx[:, :], found[:, 1, :]))


def shared1(nc, g, io):
    ctx = ExitStack()
    with ctx:
        def one(name, shape, dt):
            return ctx.enter_context(nc.sbuf_tensor(f"s1_{name}", shape, dt))

        def sb(name, shape, dt):
            return [one(f"{name}{u}", shape, dt) for u in range(2)]

        sem = semaphores(nc, ctx, "s1")
        wg, wu, wd = g.shared_w
        sil, mid = sb("sil", [P, S], fp32), sb("mid", [P, S], fp32)
        m = one("m_h", [P, SFT, S], f32r), one("m_l", [P, SFT, S], f32r)
        rows = one("rows", [P, 4, D], fp32)
        spare = one("spare_rows", [P, D], fp32)
        rows_in, rows_out, spare_ready, spare_out = [sem(n) for n in "rows_in rows_out spare_ready spare_out".split()]
        g_ready, u_ready, sil_ready, mid_ready, m_hi, m_lo, o_ready, res_ready = [sem(n) for n in "g_ready u_ready sil_ready mid_ready m_hi m_lo o_ready res_ready".split()]
        gbank, ubank, obank = g.bank[0:2], g.bank[2:4], g.bank[4:6]

        with nc.Block() as block:
            @block.sync
            def _(sp):
                sp.wait_ge(spare_ready, 1)
                sp.dma_start(io["out"][T:T + P, :], spare[:, :]).then_inc(spare_out, 16)
                sp.sem_inc(rows_out, 16)
                with sp.Fori(0, B) as b:
                    sp.wait_ge(rows_out, (b + 1) * 16)
                    sp.dma_start(rows[:, :, :], g.x3_dram[bass.ds(b * S, S), :].rearrange("(t p) n -> p t n", p=P)).then_inc(rows_in, 16)
                    sp.wait_ge(res_ready, at(b, 4, 3))
                    sp.dma_start(io["out"][bass.ds(b * S, S), :].rearrange("(t p) n -> p t n", p=P), rows[:, :, :]).then_inc(rows_out, 16)
                sp.wait_ge(rows_out, 16 * (B + 1))
                sp.wait_ge(spare_out, 16)

            @block.gpsimd
            def _(gp):
                gp.memset(spare[:, :], 0.0).then_inc(spare_ready, 1)

            @block.scalar
            def _(act):
                with act.Fori(0, B) as b:
                    for c in range(SFT):
                        act.wait_ge(g_ready, at(b, SFT, c))
                        act.activation(sil[c % 2][:, :], gbank[c % 2][:, :], ACT.Silu).then_inc(sil_ready, 1)
                        act.wait_ge(mid_ready, at(b, SFT, c))
                        act.activation(m[0][:, c, :], mid[c % 2][:, :], ACT.Copy).then_inc(m_hi, 1)

            @block.tensor
            def _(pe):
                def batch(b):
                    def xT(k):
                        return [x[:, k, bass.ds(b * S, S)] for x in (g.xT_h, g.xT_l)]

                    for c in range(SFT):
                        if c >= 2:
                            pe.wait_ge(mid_ready, at(b, SFT, c - 2))
                        for w, bank, ready in ((wg, gbank, g_ready), (wu, ubank, u_ready)):
                            for k in range(KD):
                                last = mm3(pe, bank[c % 2][:, :], [x[:, k, c * P:(c + 1) * P] for x in w], xT(k), k == 0, k == KD - 1)
                            last.then_inc(ready, 1)
                    for t in range(4):
                        if t >= 2:
                            pe.wait_ge(res_ready, at(b, 4, t - 2))
                        for c in range(SFT):
                            if t == 0:
                                pe.wait_ge(m_lo, at(b, SFT, c))
                            last = mm3(pe, obank[t % 2][:, :], [x[:, c, t * P:(t + 1) * P] for x in m], [x[:, c, :] for x in wd], c == 0, c == SFT - 1)
                        last.then_inc(o_ready, 1)

                with pe.Fori(0, B) as b:
                    batch(b)

            @block.vector
            def _(v):
                with v.Fori(0, B) as b:
                    for c in range(SFT):
                        v.wait_ge(sil_ready, at(b, SFT, c))
                        v.wait_ge(u_ready, at(b, SFT, c))
                        v.tensor_tensor(mid[c % 2][:, :], ubank[c % 2][:, :], sil[c % 2][:, :], ALU.mult).then_inc(mid_ready, 1)
                        v.wait_ge(m_hi, at(b, SFT, c))
                        v.tensor_tensor(m[1][:, c, :], mid[c % 2][:, :], f(m[0][:, c, :]), ALU.subtract).then_inc(m_lo, 1)
                    v.wait_ge(rows_in, (b + 1) * 16)
                    for t in range(4):
                        v.wait_ge(o_ready, at(b, 4, t))
                        v.tensor_tensor(rows[:, t, :], obank[t % 2][:, :], rows[:, t, :], ALU.add).then_inc(res_ready, 1)


def experts1(nc, g, io):
    PAIRS = E1 // 2
    ctx = ExitStack()
    with ctx:
        def one(name, shape, dt):
            return ctx.enter_context(nc.sbuf_tensor(f"e1_{name}", shape, dt))

        def sb(name, shape, dt):
            return [one(f"{name}{u}", shape, dt) for u in range(2)]

        sem = semaphores(nc, ctx, "e1")

        def sem2(name):
            return [sem(f"{name}{u}") for u in range(2)]

        raw_g, raw_u, raw_d = sb("raw_g", [P, KD * FF], fp32), sb("raw_u", [P, KD * FF], fp32), sb("raw_d", [P, FT, D], fp32)
        wg, wu, wd = [list(zip(sb(n + "_h", s, f32r), sb(n + "_l", s, f32r))) for n, s in (("wg", [P, KD * FF]), ("wu", [P, KD * FF]), ("wd", [P, FT, D]))]
        idx_in, idx_out = [sb(f"idx_in{t}", [P, 1], i32) for t in range(2)], [sb(f"idx_out{t}", [P, 1], i32) for t in range(2)]
        xg = [sb(f"xg{t}", [P, D], fp32) for t in range(2)]
        xT = list(zip(sb("xT_h", [P, KD, CAP], f32r), sb("xT_l", [P, KD, CAP], f32r)))
        sil, mid = sb("sil", [P, CAP], fp32), sb("mid", [P, CAP], fp32)
        m = list(zip(sb("m_h", [P, FT, CAP], f32r), sb("m_l", [P, FT, CAP], f32r)))
        y = [sb(f"y{t}", [P, D], fp32) for t in range(2)]

        passed = {"pool": sem("passed_pool")}
        raw_in, idx_step, arrived, xT_ready, x_hi, x_lo = sem2("raw_in"), sem2("idx_step"), sem2("arrived"), sem2("xT_ready"), sem2("x_hi"), sem2("x_lo")
        w_hi, w_lo = [sem2(f"w_hi_{n}") for n in "gud"], [sem2(f"w_lo_{n}") for n in "gud"]
        gu_ready, sil_ready, mid_ready, m_hi, m_lo = [sem(n) for n in "gu_ready sil_ready mid_ready m_hi m_lo".split()]
        o_ready, y_ready, y_free, added, out_step = sem2("o_ready"), sem2("y_ready"), sem2("y_free"), sem2("added"), sem2("out_step")
        xbank, hbank, obank = g.bank[0:2], g.bank[2:4], g.bank[4:6]
        ROWS = [P, P, FLAST]

        def turns(eng, turn, peel_first=False):
            if peel_first:
                turn(0)
            with eng.Fori(int(peel_first), PAIRS - 1) as i:
                turn(i)
            turn(PAIRS - 1)

        def following(i, u):
            return (i, 1) if u == 0 else (i + 1, 0)

        def exists(e):
            return not isinstance(e[0], int) or e[0] < PAIRS

        def seq(i, u, c):
            return i * (2 * FT) + (u * FT + c + 1)

        with nc.Block() as block:
            @block.sync
            def _(sp):
                def load(i, u):
                    e = i * 2 + u
                    sp.dma_start(raw_g[u][:, :], io["ew_gate"][bass.ds(e, 1), :, :, :].rearrange("a p k n -> (a p) (k n)")).then_inc(raw_in[u], 16)
                    sp.dma_start(raw_u[u][:, :], io["ew_up"][bass.ds(e, 1), :, :, :].rearrange("a p k n -> (a p) (k n)")).then_inc(raw_in[u], 16)
                    sp.dma_start(raw_d[u][:, 0:2, :], io["ew_down"][bass.ds(e, 1), 0:2 * P, :].rearrange("a (k p) n -> p (a k) n", p=P)).then_inc(raw_in[u], 16)
                    sp.dma_start(raw_d[u][0:FLAST, 2, :], io["ew_down"][bass.ds(e, 1), 2 * P:FF, :].rearrange("a p n -> (a p) n")).then_inc(raw_in[u], 16)

                load(0, 0)
                load(0, 1)
                with sp.Fori(1, PAIRS) as i:
                    for u in range(2):
                        for part in w_lo:
                            sp.wait_ge(part[u], i)
                        load(i, u)

            @block.gpsimd
            def _(gp):
                def fetch(i, u):
                    if not isinstance(i, int) or i > 0:
                        gp.wait_ge(xT_ready[u], i)
                    for t in range(2):
                        ins = gp.tensor_copy(idx_in[t][u][:, :], g.gather_idx[:, bass.ds(i * 4 + (2 * u + t), 1)])
                    ins.then_inc(idx_step[u], 1)
                    gp.wait_ge(idx_step[u], i + 1)
                    gp.sem_inc(passed["pool"], 1)
                    for t in range(2):
                        gp.indirect_dma_start(xg[t][u][:, :], None, g.xn_dram, bass.IndirectOffsetOnAxis(idx_in[t][u][:, 0:1], 0)).then_inc(arrived[u], 16)

                def add(i, u):
                    for t in range(2):
                        ins = gp.tensor_copy(idx_out[t][u][:, :], g.scatter_idx[:, bass.ds(i * 4 + (2 * u + t), 1)])
                    ins.then_inc(out_step[u], 1)
                    gp.wait_ge(out_step[u], i + 1)
                    if u:
                        gp.wait_ge(added[0], (i + 1) * 32)
                    elif not isinstance(i, int) or i > 0:
                        gp.wait_ge(added[1], i * 32)
                    gp.sem_inc(y_free[1 - u], 1)
                    gp.wait_ge(y_ready[u], i + 1)
                    gp.sem_inc(passed["pool"], 1)
                    for t in range(2):
                        gp.indirect_dma_start(io["out"], bass.IndirectOffsetOnAxis(idx_out[t][u][:, 0:1], 0), y[t][u][:, :], None,
                                              compute_op=ALU.add).then_inc(added[u], 16)

                gp.sem_inc(y_free[0], 1)
                fetch(0, 0)

                def turn(i):
                    for u in range(2):
                        if exists(following(i, u)):
                            fetch(*following(i, u))
                        add(i, u)

                turns(gp, turn, True)
                for u in range(2):
                    gp.wait_ge(added[u], 32 * PAIRS)

            @block.scalar
            def _(act):
                def split_w(e, part):
                    if not exists(e):
                        return
                    i, u = e
                    act.wait_ge(raw_in[u], (i + 1) * 64)
                    if part < 2:
                        raw, w = ((raw_g, wg), (raw_u, wu))[part]
                        act.activation(w[u][0][:, :], raw[u][:, :], ACT.Copy).then_inc(w_hi[part][u], 1)
                    else:
                        act.activation(wd[u][0][:, 0:2, :], raw_d[u][:, 0:2, :], ACT.Copy)
                        act.activation(wd[u][0][0:FLAST, 2, :], raw_d[u][0:FLAST, 2, :], ACT.Copy).then_inc(w_hi[2][u], 1)

                def split_x(e):
                    if not exists(e):
                        return
                    i, u = e
                    act.wait_ge(xT_ready[u], i + 1)
                    for t in range(2):
                        ins = act.activation(xT[u][0][:, :, t * P:(t + 1) * P], xbank[t][:, :].rearrange("p (k n) -> p k n", n=P), ACT.Copy)
                    ins.then_inc(x_hi[u], 1)

                for part in range(3):
                    split_w((0, 0), part)
                split_x((0, 0))

                def turn(i):
                    for u in range(2):
                        for c in range(FT):
                            r = ROWS[c]
                            act.wait_ge(gu_ready, seq(i, u, c))
                            act.activation(sil[c % 2][0:r, :], hbank[c % 2][0:r, 0:CAP], ACT.Silu).then_inc(sil_ready, 1)
                            act.wait_ge(mid_ready, seq(i, u, c))
                            act.activation(m[u][0][0:r, c, :], mid[c % 2][0:r, :], ACT.Copy).then_inc(m_hi, 1)
                            if c < 2:
                                split_w(following(i, u), c)
                        split_x(following(i, u))
                        split_w(following(i, u), 2)
                        act.wait_ge(o_ready[u], i + 1)
                        act.wait_ge(y_free[u], i + 1)
                        for t in range(2):
                            ins = act.activation(y[t][u][:, :], obank[t][:, :], ACT.Copy, scale=g.slot_weight[:, bass.ds(i * 4 + (2 * u + t), 1)])
                        ins.then_inc(y_ready[u], 1)

                turns(act, turn)

            @block.tensor
            def _(pe):
                def turn_x(e):
                    if not exists(e):
                        return
                    i, u = e
                    pe.wait_ge(arrived[u], (i + 1) * 32)
                    for t in range(2):
                        for k in range(KD):
                            last = pe.transpose(xbank[t][:, k * P:(k + 1) * P], xg[t][u][:, k * P:(k + 1) * P], g.ident[:, :])
                    last.then_inc(xT_ready[u], 1)

                turn_x((0, 0))

                def turn(i):
                    for u in range(2):
                        pe.wait_ge(x_lo[u], i + 1)
                        for c in range(FT):
                            r = ROWS[c]
                            if c >= 2:
                                pe.wait_ge(mid_ready, seq(i, u, c - 2))
                            for n, w in enumerate((wg[u], wu[u])):
                                if c == 0:
                                    pe.wait_ge(w_lo[n][u], i + 1)
                                for k in range(KD):
                                    last = mm3(pe, hbank[c % 2][0:r, n * CAP:(n + 1) * CAP], [x[:, k * FF + c * P:k * FF + c * P + r] for x in w],
                                               [x[:, k, :] for x in xT[u]], k == 0, k == KD - 1)
                            last.then_inc(gu_ready, 1)
                        turn_x(following(i, u))
                        pe.wait_ge(w_lo[2][u], i + 1)
                        if u or not isinstance(i, int) or i > 0:
                            pe.wait_ge(y_ready[1 - u], i + u)
                        for t in range(2):
                            for c in range(FT):
                                r = ROWS[c]
                                if t == 0:
                                    pe.wait_ge(m_lo, seq(i, u, c))
                                last = mm3(pe, obank[t][:, :], [x[0:r, c, t * P:(t + 1) * P] for x in m[u]], [x[0:r, c, :] for x in wd[u]], c == 0, c == FT - 1)
                        last.then_inc(o_ready[u], 1)

                turns(pe, turn, True)

            @block.vector
            def _(v):
                def split_w(e, part):
                    if not exists(e):
                        return
                    i, u = e
                    v.wait_ge(w_hi[part][u], i + 1)
                    if part < 2:
                        raw, w = ((raw_g, wg), (raw_u, wu))[part]
                        v.tensor_tensor(w[u][1][:, :], raw[u][:, :], f(w[u][0][:, :]), ALU.subtract).then_inc(w_lo[part][u], 1)
                    else:
                        v.tensor_tensor(wd[u][1][:, 0:2, :], raw_d[u][:, 0:2, :], f(wd[u][0][:, 0:2, :]), ALU.subtract)
                        v.tensor_tensor(wd[u][1][0:FLAST, 2, :], raw_d[u][0:FLAST, 2, :], f(wd[u][0][0:FLAST, 2, :]), ALU.subtract).then_inc(w_lo[2][u], 1)

                def split_x(e):
                    if not exists(e):
                        return
                    i, u = e
                    v.wait_ge(x_hi[u], i + 1)
                    for t in range(2):
                        ins = v.tensor_tensor(xT[u][1][:, :, t * P:(t + 1) * P], xbank[t][:, :].rearrange("p (k n) -> p k n", n=P),
                                              f(xT[u][0][:, :, t * P:(t + 1) * P]), ALU.subtract)
                    ins.then_inc(x_lo[u], 1)

                for part in range(3):
                    split_w((0, 0), part)
                split_x((0, 0))

                def turn(i):
                    for u in range(2):
                        for c in range(FT):
                            r = ROWS[c]
                            v.wait_ge(sil_ready, seq(i, u, c))
                            v.tensor_tensor(mid[c % 2][0:r, :], hbank[c % 2][0:r, CAP:2 * CAP], sil[c % 2][0:r, :], ALU.mult).then_inc(mid_ready, 1)
                            v.wait_ge(m_hi, seq(i, u, c))
                            v.tensor_tensor(m[u][1][0:r, c, :], mid[c % 2][0:r, :], f(m[u][0][0:r, c, :]), ALU.subtract).then_inc(m_lo, 1)
                            if c < 2:
                                split_w(following(i, u), c)
                        split_x(following(i, u))
                        split_w(following(i, u), 2)

                turns(v, turn)


def program(nc, io):
    g = Shared()
    with ExitStack() as ctx:
        def keep(stack, name, shape, dt):
            return stack.enter_context(nc.sbuf_tensor(name, shape, dt))

        constants(nc, g, ctx)
        g.summ_dram = nc.dram_tensor("summaries", [B, 2, P, 2 * KD * P], fp32, kind="Internal").ap()
        g.sorted_y = nc.dram_tensor("sorted_y", [SORTED * P, D], fp32, kind="Internal").ap()
        w3 = [P, 3 * HID * KD]
        with ExitStack() as contexts:
            g.ctx_h = keep(contexts, "ctx_h_all", [P, B, KD * S], f32r)
            g.ctx_l = keep(contexts, "ctx_l_all", [P, B, KD * S], f32r)
            front(nc, g, io)
            g.w3 = nc.alloc_sbuf_tensor_at("w3", w3, bf16, offset=(nc.sbuf_usable_end - 2 * w3[1]) // 64 * 64)
            experts0(nc, g, io)
        g.logits = keep(ctx, "logits", [P, TT, E1], fp32)
        g.gather_idx = keep(ctx, "gather_idx", [P, SLOTS], i32)
        g.scatter_idx = keep(ctx, "scatter_idx", [P, SLOTS], i32)
        g.slot_weight = keep(ctx, "slot_weight", [P, SLOTS], fp32)
        g.xn_dram = nc.dram_tensor("xn_rows", [T, D], fp32, kind="Internal").ap()
        g.x3_dram = nc.dram_tensor("x3_rows", [T, D], fp32, kind="Internal").ap()
        with ExitStack() as turned:
            g.xT_h = keep(turned, "xT_h", [P, KD, T], f32r)
            g.xT_l = keep(turned, "xT_l", [P, KD, T], f32r)
            with ExitStack() as rows:
                g.rows = keep(rows, "rows", [P, TT, D], fp32)
                ffn0(nc, g, io)
                attention1(nc, g, io)
            g.shared_w = [[keep(turned, f"s1_{n}_{part}", [P, k, width], f32r) for part in ("h", "l")]
                          for n, k, width in (("wg", KD, SFT * P), ("wu", KD, SFT * P), ("wd", SFT, D))]
            route1(nc, g, io)
            shared1(nc, g, io)
        experts1(nc, g, io)
def laid_out(inputs):
    a = {n: np.asarray(x) for n, x in inputs.items()}
    def chunks(w):
        return w.reshape(w.shape[0], -1, P).transpose(2, 1, 0)
    def rows(w):
        return w.reshape(-1, P, w.shape[1]).transpose(1, 0, 2)
    o = {
        "x": a["x"].reshape(T, D),
        "tokens": a["itok_BxS_13_99985"].reshape(TT, P).T,
        "ctx": a["ctx_2048"].reshape(B, S, KD, P).transpose(3, 0, 2, 1),
        "norm_w": a["L0_ffn_norm_w"].reshape(1, D),
        "wffn": np.concatenate([chunks(a["L0_ffn_w_gv"]).reshape(P, -1), chunks(a["L0_ffn_w_out"]).reshape(P, -1)], axis=1),
        "wq": chunks(a["L1_xattn_Wq"]),
        "wg": chunks(a["L1_xattn_Wg"]),
        "bg": a["L1_xattn_bg"].reshape(KD, P).T,
        "wkv": chunks(a["L1_xattn_Wkv"]),
        "wo": chunks(a["L1_xattn_Wo"]),
        "router": chunks(a["L1_ffn_gate_w"]),
        "ew_gate": a["L1_ffn_w_gate"].reshape(E1, KD, P, FF).transpose(0, 2, 1, 3),
        "ew_up": a["L1_ffn_w_up"].reshape(E1, KD, P, FF).transpose(0, 2, 1, 3),
        "ew_down": a["L1_ffn_w_down"],
        "sw_gate": rows(a["L1_ffn_sw_gate"]),
        "sw_up": rows(a["L1_ffn_sw_up"]),
        "sw_down": a["L1_ffn_sw_down"],
    }
    return {n: np.ascontiguousarray(x) for n, x in o.items()}


def kernel(**inputs):
    import concourse.bacc as bacc
    from concourse.bass_utils import run_bass_kernel_spmd
    nc = bacc.Bacc("TRN2", target_bir_lowering=False, num_devices=1)
    arrays = laid_out(inputs)
    io = {n: nc.dram_tensor(f"in_{n}", x.shape, mybir.dt.from_np(x.dtype), kind="ExternalInput").ap() for n, x in arrays.items()}
    io["out"] = nc.dram_tensor("out", (T + P, D), fp32, kind="ExternalOutput").ap()
    program(nc, io)
    r = run_bass_kernel_spmd(nc, [{f"in_{n}": x for n, x in arrays.items()}], core_ids=[0])
    return r.results[0]["out"][0:T].reshape(B, S, D)
```
